# Optimizing a Trainium2 kernel written in Bass

```python
import numpy as np
import jax
import jax.numpy as jnp

def _softmax(x, axis=-1):
    return jax.nn.softmax(x, axis=axis)

def _gelu(x):
    return jax.nn.gelu(x, approximate=True)

def _silu(x):
    return jax.nn.silu(x)

def _sigmoid(x):
    return jax.nn.sigmoid(x)

def _layernorm(x, axis=-1, eps=1e-05):
    m = jnp.mean(x, axis=axis, keepdims=True)
    v = jnp.var(x, axis=axis, keepdims=True)
    return (x - m) / jnp.sqrt(v + eps)

def _scatter_add(tgt, idx, src, axis=0):
    return tgt.at[idx].add(src)

def _segment_sum(src, seg, n):
    return jax.ops.segment_sum(src, seg, n)
kernel_name = 'mk_perceiver_d1_seqx_r4_5c6122'

def setup_inputs(seed: int=0):
    np.random.seed(seed)
    _w = jnp.asarray

    def _rec_inputs():
        import jax
        import jax.numpy as jnp
        _rk = jax.random.key(seed)
        x = -0.0002928 + 1 * jax.random.normal(jax.random.fold_in(_rk, 1), (8, 64, 256), jnp.float32)
        _lenS = 64 - jax.random.randint(jax.random.fold_in(_rk, 7), (8,), 0, max(1, 64 // 4) + 1, jnp.int32)
        _lenS2 = 1601 - jax.random.randint(jax.random.fold_in(_rk, 8), (8,), 0, max(1, 1601 // 4) + 1, jnp.int32)
        _ctx_1024P = jax.random.normal(jax.random.fold_in(_rk, 11), (8, 16, 256), jnp.float32)
        _ctx_1024c = jax.random.dirichlet(jax.random.fold_in(_rk, 511), 0.3 * jnp.ones((16,), jnp.float32), (8, 1601))
        _ctx_1024t = jnp.einsum('bsk,bkd->bsd', _ctx_1024c, _ctx_1024P)
        _ctx_1024t = _ctx_1024t * jax.lax.rsqrt(jnp.mean(jnp.square(_ctx_1024t)) + 1e-12) * 0.953939
        ctx_1024 = -1.39393e-06 + 0.999914 * (_ctx_1024t + 0.3 * jax.random.normal(jax.random.fold_in(_rk, 611), (8, 1601, 256), jnp.float32))
        return (x, ctx_1024)
    x, ctx_1024 = _rec_inputs()

    def _L0_xattn_setup():
        import jax, jax.numpy as jnp
        import numpy as np
        D_MODEL = 256
        NUM_HEADS = 16
        D_K = D_MODEL // NUM_HEADS
        key = jax.random.key(seed)
        ks = jax.random.split(key, 11)
        B, S = (2, 512)
        scale = 1.0 / np.sqrt(D_MODEL)
        inp = {'q': jax.random.normal(ks[0], (B, S, D_MODEL), jnp.float32), 'k': jax.random.normal(ks[1], (B, S, D_MODEL), jnp.float32), 'v': jax.random.normal(ks[2], (B, S, D_MODEL), jnp.float32), 'Wq': jax.random.normal(ks[3], (D_MODEL, D_MODEL), jnp.float32) * scale, 'bq': jax.random.normal(ks[4], (D_MODEL,), jnp.float32) * 0.01, 'Wk': jax.random.normal(ks[5], (D_MODEL, D_MODEL), jnp.float32) * scale, 'bk': jax.random.normal(ks[6], (D_MODEL,), jnp.float32) * 0.01, 'Wv': jax.random.normal(ks[7], (D_MODEL, D_MODEL), jnp.float32) * scale, 'bv': jax.random.normal(ks[8], (D_MODEL,), jnp.float32) * 0.01, 'Wo': jax.random.normal(ks[9], (D_MODEL, D_MODEL), jnp.float32) * scale, 'bo': jax.random.normal(ks[10], (D_MODEL,), jnp.float32) * 0.01}
        return inp
    _L0_xattn_all = _L0_xattn_setup()
    _L0_xattn_in = {k: v for k, v in _L0_xattn_all.items() if k in ('Wq', 'bq', 'Wk', 'bk', 'Wv', 'bv', 'Wo', 'bo')}
    del _L0_xattn_all

    def _L0_attn_setup():
        import jax, jax.numpy as jnp
        import numpy as np
        import math
        B, T, E, H = (4, 512, 256, 16)
        D = E // H
        rng = jax.random.key(seed)
        k1, k2, k3, k4, k5 = jax.random.split(rng, 5)
        scale_w = 1.0 / math.sqrt(E)
        return {'query': jax.random.normal(k1, (B, T, E), jnp.float32), 'key': jax.random.normal(k2, (B, T, E), jnp.float32), 'value': jax.random.normal(k3, (B, T, E), jnp.float32), 'in_proj_weight': jax.random.normal(k4, (3 * E, E), jnp.float32) * scale_w, 'out_proj_weight': jax.random.normal(k5, (E, E), jnp.float32) * scale_w}
    _L0_attn_all = _L0_attn_setup()
    _L0_attn_in = {k: v for k, v in _L0_attn_all.items() if k in ('key', 'value', 'in_proj_weight', 'out_proj_weight')}
    del _L0_attn_all

    def _L0_ffn_setup():
        import jax, jax.numpy as jnp
        import numpy as np
        D = 256
        H = 1024
        E = 8
        K = 2
        B, S = (4, 512)
        key = jax.random.key(seed)
        ks = jax.random.split(key, 8)

        def lin(k, fan_in, shape):
            bound = 1.0 / np.sqrt(fan_in)
            return jax.random.uniform(k, shape, jnp.float32, -bound, bound)
        return {'x': jax.random.normal(ks[0], (B, S, D), jnp.float32), 'Wg': lin(ks[1], D, (D, E)), 'bg': lin(ks[2], D, (E,)), 'W1': lin(ks[3], D, (E, D, H)), 'b1': lin(ks[4], D, (E, H)), 'W2': lin(ks[5], H, (E, H, D)), 'b2': lin(ks[6], H, (E, D))}
    _L0_ffn_all = _L0_ffn_setup()
    _L0_ffn_in = {k: v for k, v in _L0_ffn_all.items() if k in ('Wg', 'bg', 'W1', 'b1', 'W2', 'b2')}
    del _L0_ffn_all
    return {'x': x, 'ctx_1024': ctx_1024, 'L0_xattn_Wq': _L0_xattn_in['Wq'], 'L0_xattn_bq': _L0_xattn_in['bq'], 'L0_xattn_Wk': _L0_xattn_in['Wk'], 'L0_xattn_bk': _L0_xattn_in['bk'], 'L0_xattn_Wv': _L0_xattn_in['Wv'], 'L0_xattn_bv': _L0_xattn_in['bv'], 'L0_xattn_Wo': _L0_xattn_in['Wo'], 'L0_xattn_bo': _L0_xattn_in['bo'], 'L0_attn_key': _L0_attn_in['key'], 'L0_attn_value': _L0_attn_in['value'], 'L0_attn_in_proj_weight': _L0_attn_in['in_proj_weight'], 'L0_attn_out_proj_weight': _L0_attn_in['out_proj_weight'], 'L0_ffn_Wg': _L0_ffn_in['Wg'], 'L0_ffn_bg': _L0_ffn_in['bg'], 'L0_ffn_W1': _L0_ffn_in['W1'], 'L0_ffn_b1': _L0_ffn_in['b1'], 'L0_ffn_W2': _L0_ffn_in['W2'], 'L0_ffn_b2': _L0_ffn_in['b2']}

def reference(x, ctx_1024, L0_xattn_Wq, L0_xattn_bq, L0_xattn_Wk, L0_xattn_bk, L0_xattn_Wv, L0_xattn_bv, L0_xattn_Wo, L0_xattn_bo, L0_attn_key, L0_attn_value, L0_attn_in_proj_weight, L0_attn_out_proj_weight, L0_ffn_Wg, L0_ffn_bg, L0_ffn_W1, L0_ffn_b1, L0_ffn_W2, L0_ffn_b2):
    import jax
    import jax.numpy as jnp

    def _L0_xattn_ref(q, k, v, Wq, bq, Wk, bk, Wv, bv, Wo, bo):
        import jax, jax.numpy as jnp
        import numpy as np
        D_MODEL = 256
        NUM_HEADS = 16
        D_K = D_MODEL // NUM_HEADS
        B, S, _ = q.shape

        def proj(x, W, b):
            y = x @ W.T + b
            return y.reshape(B, -1, NUM_HEADS, D_K).transpose(0, 2, 1, 3)
        qh = proj(q, Wq, bq)
        kh = proj(k, Wk, bk)
        vh = proj(v, Wv, bv)
        scores = jnp.einsum('bhqd,bhkd->bhqk', qh, kh) / np.sqrt(D_K)
        attn = jax.nn.softmax(scores, axis=-1)
        out = jnp.einsum('bhqk,bhkd->bhqd', attn, vh)
        out = out.transpose(0, 2, 1, 3).reshape(B, S, D_MODEL)
        return out @ Wo.T + bo

    def _L0_attn_ref(query, key, value, in_proj_weight, out_proj_weight):
        import jax, jax.numpy as jnp
        import numpy as np
        import math
        B, T, E, H = (4, 512, 256, 16)
        D = E // H
        b, t, e = query.shape
        qkv = jnp.einsum('bte,fe->btf', query, in_proj_weight).reshape(b, t, 3, H, D)
        q = jnp.transpose(qkv[:, :, 0], (0, 2, 1, 3))
        k = jnp.transpose(qkv[:, :, 1], (0, 2, 1, 3))
        v = jnp.transpose(qkv[:, :, 2], (0, 2, 1, 3))
        q = q / math.sqrt(D)
        scores = jnp.einsum('bhqd,bhkd->bhqk', q, k)
        pos = jnp.arange(t)
        causal = pos[:, None] >= pos[None, :]
        scores = jnp.where(causal[None, None], scores, jnp.float32(-jnp.inf))
        attn = jax.nn.softmax(scores, axis=-1)
        out = jnp.einsum('bhqk,bhkd->bhqd', attn, v)
        out = jnp.transpose(out, (0, 2, 1, 3)).reshape(b, t, e)
        out = jnp.einsum('bte,fe->btf', out, out_proj_weight)
        return out

    def _L0_ffn_ref(x, Wg, bg, W1, b1, W2, b2):
        import jax, jax.numpy as jnp
        import numpy as np
        D = 256
        H = 1024
        E = 8
        K = 2
        B, S = (4, 512)
        B_, S_, D_ = x.shape
        xt = x.reshape(-1, D_)
        logits = xt @ Wg + bg
        scores = jax.nn.softmax(logits, axis=-1)
        topk_probs, topk_idx = jax.lax.top_k(scores, K)
        h = jnp.einsum('nd,edh->enh', xt, W1) + b1[:, None, :]
        h = jax.nn.gelu(h, approximate=False)
        eo = jnp.einsum('enh,ehd->end', h, W2) + b2[:, None, :]
        eo = jnp.transpose(eo, (1, 0, 2))
        sel = jnp.take_along_axis(eo, topk_idx[:, :, None], axis=1)
        out = jnp.einsum('nk,nkd->nd', topk_probs, sel)
        return out.reshape(B_, S_, D_)
    x = x + _L0_xattn_ref(_layernorm(x, axis=-1), ctx_1024, ctx_1024, L0_xattn_Wq, L0_xattn_bq, L0_xattn_Wk, L0_xattn_bk, L0_xattn_Wv, L0_xattn_bv, L0_xattn_Wo, L0_xattn_bo)
    x = x + _L0_attn_ref(_layernorm(x, axis=-1), L0_attn_key, L0_attn_value, L0_attn_in_proj_weight, L0_attn_out_proj_weight)
    x = x + _L0_ffn_ref(_layernorm(x, axis=-1), L0_ffn_Wg, L0_ffn_bg, L0_ffn_W1, L0_ffn_b1, L0_ffn_W2, L0_ffn_b2)
    return x

_drawn_inputs = setup_inputs


def setup_inputs(seed=0):
    import zlib

    import numpy as np

    out = dict(_drawn_inputs(seed))
    spreads = {}
    factors = {'L0_xattn_bq': 23.216,
     'L0_xattn_bk': 64.0,
     'L0_xattn_bv': 5.223,
     'L0_xattn_bo': 4.869,
     'L0_ffn_bg': 6.665,
     'L0_ffn_b1': 8.0,
     'L0_ffn_b2': 8.0}
    for name, (base, spread) in spreads.items():
        noise = np.random.default_rng([zlib.crc32(name.encode()), seed]).standard_normal(out[name].shape)
        drawn = base * np.exp(spread * noise) if base else spread * noise
        out[name] = jnp.asarray(drawn.astype(out[name].dtype))
    for name, factor in factors.items():
        out[name] = (out[name] * factor).astype(out[name].dtype)
    return out
```

```python
from contextlib import ExitStack

import concourse.bass as bass
from concourse import mybir

F32 = mybir.dt.float32
F32R = mybir.dt.float32r
BF16 = mybir.dt.bfloat16
ACT = mybir.ActivationFunctionType
ALU = mybir.AluOpType
AX = mybir.AxisListType
PE_ENGINE = mybir.EngineType.PE

P = 128
B, Q, D = 8, 64, 256
S = 1601
H, DK = 16, 16
DC = D // P
HG = P // DK
G = H // HG
PAIRS = HG // 2
TOK = B * Q
TT = TOK // P
KT = -(-S // P)
ROWS = [min(P, S - P * k) for k in range(KT)]
CW = 402
CH = [0, 400, 800, S - CW]
NC = len(CH)
EDGE = [0] + [c + CW for c in CH]
HALVES = NC // 2
E, HID = 8, 1024
HC = HID // P
EPS = 1e-5
SCALE = 0.25
FAR = -1e30

K_UNITS = G * NC
M_UNITS = G * PAIRS * HALVES
SPLIT_AT = {0: [0, 1], 1: [2], 2: [3]}
K_AT = {1: [0, 1], 2: [2, 3], 3: [4, 5], 4: [6, 7]}
V_AT = {k: [k - 1] for k in range(1, KT - 1)} | {KT - 1: [KT - 2, KT - 1]}
M_AT = {k: [2 * (k - 5), 2 * (k - 5) + 1] for k in range(5, 13)}
PROJ_UNITS = K_UNITS + KT
CONST_DMAS = 9
CONSTS_MADE = 7
TILE_LINKS = 33


def unit_order():
    order = []
    for k in range(KT):
        order += [("k", u) for u in K_AT.get(k, [])] + [("v", u) for u in V_AT.get(k, [])]
    return {unit: n for n, unit in enumerate(order)}


ORDER = unit_order()


def perceiver_kernel(nc, x, ctx_t, w_t, wg_t, biases, bo_row, bg_row, w1, b1, w2, b2, eye, masks, causal, out):
    stack = ExitStack()
    with stack:
        def sem(name):
            return stack.enter_context(nc.semaphore(name))

        def sb(name, shape, dt=F32, where=stack):
            return where.enter_context(nc.sbuf_tensor(name, shape, dt))

        ident = sb("ident", [P, P])
        ones_bf = sb("ones_bf", [P, P], BF16)
        ident_bf = sb("ident_bf", [P, P], BF16)
        ones_f = sb("ones_f", [P, P])
        zero = sb("zero", [P, 1])
        neg_half = sb("neg_half", [P, 1])
        mask_sb = sb("mask_sb", [P, HG + 2])
        bias_sb = sb("bias_sb", [P, 3, DC])
        bq_scaled = sb("bq_scaled", [P, DC])
        bo_sb = sb("bo_sb", [1, D])
        bg_sb = sb("bg_sb", [1, E])
        wg_sb = sb("wg_sb", [P, DC, E])
        b1_sb = sb("b1_sb", [P, E, HC])
        b2_sb = sb("b2_sb", [E, D])
        x_all = sb("x_all", [P, TT, D])
        xn2_t = sb("xn2_t", [P, DC, TOK])
        gates = sb("gates", [P, TT, E])

        attn = ExitStack()
        with attn:
            w_sb = sb("w_sb", [P, 6, DC, D], F32, attn)
            wk_hi = sb("wk_hi", [P, DC, D], F32R, attn)
            wk_lo = sb("wk_lo", [P, DC, D], F32R, attn)
            wv_hi = sb("wv_hi", [P, DC, D], F32R, attn)
            wv_lo = sb("wv_lo", [P, DC, D], F32R, attn)
            causal_sb = sb("causal_sb", [P, Q], F32, attn)
            causal_bf = sb("causal_bf", [P, Q], BF16, attn)
            q_hi = sb("q_hi", [P, G, TOK], F32R, attn)
            q_lo = sb("q_lo", [P, G, TOK], F32R, attn)
            ctx_raw = sb("ctx_raw", [P, DC, S], F32, attn)
            ctx_hi = sb("ctx_hi", [P, DC, S], F32R, attn)
            ctx_lo = sb("ctx_lo", [P, DC, S], F32R, attn)
            k_hi = sb("k_hi", [P, 2, G, S], F32R, attn)
            k_lo = sb("k_lo", [P, 2, G, S], F32R, attn)
            v_sb = sb("v_sb", [P, 2, KT * D], F32, attn)
            probs = sb("probs", [P, 2, G * 512], F32, attn)
            prob_sum = sb("prob_sum", [P, G * 512], F32, attn)
            qbd_hi = sb("qbd_hi", [P, 2, G, HG, Q], F32R, attn)
            qbd_lo = sb("qbd_lo", [P, 2, G, HG, Q], F32R, attn)
            maxes = sb("maxes", [P, G * PAIRS, HALVES], F32, attn)
            neg_max = sb("neg_max", [P, G * PAIRS], F32, attn)
            shift = sb("shift", [P, 2, G * PAIRS, P], BF16, attn)
            recip = sb("recip", [P, 2 * P], F32, attn)
            o_norm = sb("o_norm", [P, G, 2, Q], F32, attn)
            o_odd = sb("o_odd", [P, G, Q], F32, attn)
            o_t = sb("o_t", [P, G, P], F32, attn)
            unused = sb("unused", [P, 1], F32, attn)
            stats = sb("stats", [P, 6], F32, attn)
            mean_var = sb("mean_var", [P, 2], F32, attn)
            var_eps = sb("var_eps", [P, 1], F32, attn)
            rstd = sb("rstd", [P, 1], F32, attn)
            xn = sb("xn", [P, D], F32, attn)
            xn_t = sb("xn_t", [P, DC, P], F32, attn)
            q_tile = sb("q_tile", [P, G, P], F32, attn)
            x1 = sb("x1", [P, D], F32, attn)
            k2_t = sb("k2_t", [P, G, P], F32, attn)
            v2 = sb("v2", [P, D], F32, attn)
            o2_t = sb("o2_t", [P, G, P], F32, attn)
            logits = sb("logits", [P, E], F32, attn)
            row_max = sb("row_max", [P, 1], F32, attn)
            row_sum = sb("row_sum", [P, 1], F32, attn)
            above = sb("above", [P, E, E], F32, attn)
            ties = sb("ties", [P, E, E], F32, attn)
            rank = sb("rank", [P, E], F32, attn)
            earlier = sb("earlier", [P, E, E], F32, attn)
            gates_t = sb("gates_t", [E, P], F32, attn)
            gate_tile = sb("gate_tile", [P, E], F32, attn)
        qbd2 = v_sb[:, 1, 0:G * HG * P].rearrange("p (b g h q) -> p b g h q", b=2, g=G, h=HG)
        probs2 = v_sb[:, 1, G * HG * P:G * HG * P + G * 512]
        shift2 = prob_sum[:, :].bitcast(BF16).rearrange("p (b n c) -> p b n c", b=2, c=P)
        masked = probs[:, 0, :].rearrange("p (b n k) -> p b n k", b=2, k=Q)
        w_raw = probs[:, 0, :].rearrange("p (w c n) -> p w c n", w=2, c=DC)

        moe = ExitStack()
        with moe:
            w1_sb = [sb(f"w1_sb{i}", [P, DC, HID], F32, moe) for i in range(2)]
            w2_sb = [sb(f"w2_sb{i}", [P, HC, D], F32, moe) for i in range(2)]
            h_t = sb("h_t", [P, HC, TOK], F32, moe)

        bank = stack.enter_context(nc.psum_tensor("bank", [P, 8, 512], F32))
        SM, PROJ, O = 4, 6, 7

        def heads_of(bi_bank):
            return bi_bank.rearrange("p (g s q) -> p g s q", g=G, s=2)

        consts_in = sem("consts_in")
        weights_in = sem("weights_in")
        x_in = sem("x_in")
        ctx_in = sem("ctx_in")
        consts_made = sem("consts_made")
        raw_split = sem("raw_split")
        xn_ready = sem("xn_ready")
        var_ready = sem("var_ready")
        rstd_ready = sem("rstd_ready")
        xt_psum = sem("xt_psum")
        xt_ready = sem("xt_ready")
        q_psum = sem("q_psum")
        q_ready = sem("q_ready")
        q_split = sem("q_split")
        q_hi_done = sem("q_hi_done")
        qbd_ready = sem("qbd_ready")
        ctx_hi_done = sem("ctx_hi_done")
        ctx_lo_done = sem("ctx_lo_done")
        proj_done = sem("proj_done")
        k_hi_done = sem("k_hi_done")
        proj_free = sem("proj_free")
        max_psum = sem("max_psum")
        max_taken = sem("max_taken")
        shift_ready = sem("shift_ready")
        scores_done = sem("scores_done")
        exp_done = sem("exp_done")
        pv_done = sem("pv_done")
        summed = sem("summed")
        denom_done = sem("denom_done")
        o_ready = sem("o_ready")
        dve_step = sem("dve_step")
        y1_psum = sem("y1_psum")
        xn1_ready = sem("xn1_ready")
        xn1t_psum = sem("xn1t_psum")
        xn1t_ready = sem("xn1t_ready")
        qkv2_psum = sem("qkv2_psum")
        k2_ready = sem("k2_ready")
        q2_ready = sem("q2_ready")
        qbd2_ready = sem("qbd2_ready")
        s2_psum = sem("s2_psum")
        shift2_ready = sem("shift2_ready")
        st2_psum = sem("st2_psum")
        probs2_ready = sem("probs2_ready")
        o2_psum = sem("o2_psum")
        o2_ready = sem("o2_ready")
        y2_psum = sem("y2_psum")
        xn2_ready = sem("xn2_ready")
        xn2t_psum = sem("xn2t_psum")
        xn2t_ready = sem("xn2t_ready")
        xn2t_kept = sem("xn2t_kept")
        logits_psum = sem("logits_psum")
        negmax_ready = sem("negmax_ready")
        gexp_ready = sem("gexp_ready")
        gates_ready = sem("gates_ready")
        gatest_psum = sem("gatest_psum")
        gatest_ready = sem("gatest_ready")
        bias2_psum = sem("bias2_psum")
        tile_done = sem("tile_done")
        w_in = [sem(f"w_in{i}") for i in range(2)]
        h_psum = sem("h_psum")
        h_ready = sem("h_ready")
        y_psum = sem("y_psum")
        y_taken = sem("y_taken")
        stored = sem("stored")

        block = stack.enter_context(nc.Block())

        @block.sync
        def _(sp):
            for dst, src in ((ident[:, :], eye), (mask_sb[:, :], masks), (bias_sb[:, :, :], biases),
                             (bo_sb[:, :], bo_row), (bg_sb[:, :], bg_row), (wg_sb[:, :, :], wg_t),
                             (b1_sb[:, :, :], b1), (b2_sb[:, :], b2), (causal_sb[:, :], causal)):
                sp.dma_start(dst, src).then_inc(consts_in, 16)
            sp.dma_start(x_all[:, :, :], x).then_inc(x_in, 16)
            sp.dma_start(w_raw, w_t[:, 6:8]).then_inc(weights_in, 16)
            sp.dma_start(w_sb[:, :, :, :], w_t[:, 0:6]).then_inc(weights_in, 16)
            sp.dma_start(ctx_raw[:, :, :], ctx_t[0]).then_inc(ctx_in, 16)
            with sp.Fori(1, B) as b:
                sp.wait_ge(ctx_lo_done, b * NC)
                sp.dma_start(ctx_raw[:, :, :], ctx_t[b]).then_inc(ctx_in, 16)
            sp.wait_ge(tile_done, TT)
            for e in range(2):
                sp.dma_start(w1_sb[e][:, :, :], w1[e]).then_inc(w_in[e], 16)
                sp.dma_start(w2_sb[e][:, :, :], w2[e]).then_inc(w_in[e], 16)
            with sp.Fori(1, E // 2) as p:
                for i in range(2):
                    sp.wait_ge(y_psum, 2 * p + i - 1)
                    sp.dma_start(w1_sb[i][:, :, :], w1[2 * p + i]).then_inc(w_in[i], 16)
                    sp.dma_start(w2_sb[i][:, :, :], w2[2 * p + i]).then_inc(w_in[i], 16)
            sp.wait_ge(y_taken, E)
            sp.dma_start(out, x_all[:, :, :]).then_inc(stored, 16)
            sp.wait_ge(stored, 16)

        @block.gpsimd
        def _(pool):
            nc.gpsimd.memset(zero[:, :], 0.0).then_inc(consts_made, 1)
            nc.gpsimd.memset(neg_half[:, :], -0.5).then_inc(consts_made, 1)
            nc.gpsimd.memset(ones_bf[:, :], 1.0).then_inc(consts_made, 1)
            nc.gpsimd.memset(ones_f[:, :], 1.0).then_inc(consts_made, 1)
            pool.wait_ge(consts_made, CONSTS_MADE)
            pool.wait_ge(consts_in, CONST_DMAS * 16)

            def inverse_root(n):
                pool.wait_ge(var_ready, n)
                nc.gpsimd.tensor_tensor(rstd[:, :], var_eps[:, :], neg_half[:, :], ALU.pow).then_inc(rstd_ready, 1)

            def spread_queries(b, parity):
                for src, dst in ((q_hi, qbd_hi), (q_lo, qbd_lo)):
                    nc.gpsimd.tensor_tensor(
                        dst[:, parity],
                        src[:, :, bass.ds(b * Q, Q)].bitcast(F32).unsqueeze(2).broadcast_to([P, G, HG, Q]),
                        mask_sb[:, 0:HG].unsqueeze(1).unsqueeze(3).broadcast_to([P, G, HG, Q]),
                        ALU.mult).then_inc(qbd_ready, 1)

            def batch(b, bi, more):
                for k in range(KT):
                    n = b * KT + k
                    buf = (KT * bi + k) % 2
                    pool.wait_ge(exp_done, n + 1)
                    if k == 0:
                        if bi == 1:
                            pool.wait_ge(denom_done, b)
                        acc = zero[:, 0:1].broadcast_to([P, G * 512])
                    else:
                        pool.wait_ge(summed, n)
                        acc = prob_sum[0:ROWS[k], :]
                    nc.gpsimd.tensor_tensor(prob_sum[0:ROWS[k], :], probs[0:ROWS[k], buf, :], acc[0:ROWS[k]],
                                            ALU.add).then_inc(summed, 1)
                    if k == 1 and more:
                        spread_queries(b + 1, (bi + 1) % 2)

            with pool.Fori(1, TT + 1) as n:
                inverse_root(n)
            pool.wait_ge(q_split, TT)
            spread_queries(0, 0)

            def tile(t, last):
                for bi in range(2):
                    batch(2 * t + bi, bi, not (last and bi))
                inverse_root(TT + 2 * t + 1)
                inverse_root(TT + 2 * t + 2)

            with pool.Fori(0, TT - 1) as t:
                tile(t, False)
            tile(TT - 1, True)

        @block.scalar
        def _(act):
            def split_hi(b, c):
                if c == 0:
                    act.wait_ge(ctx_in, 16 * (b + 1))
                nc.scalar.activation(ctx_hi[:, :, EDGE[c]:EDGE[c + 1]], ctx_raw[:, :, EDGE[c]:EDGE[c + 1]],
                                     ACT.Copy).then_inc(ctx_hi_done, 1)

            def k_unit(b, u, parity):
                n = b * PROJ_UNITS + ORDER["k", u]
                c, g = divmod(u, G)
                act.wait_ge(proj_done, n + 1)
                nc.scalar.activation(k_hi[:, parity, g, EDGE[c]:EDGE[c + 1]], bank[:, PROJ, EDGE[c] - CH[c]:CW], ACT.Identity,
                                     bias=bias_sb[:, 1, g:g + 1]).then_inc(k_hi_done, 1)

            def v_unit(b, u, parity):
                n = b * PROJ_UNITS + ORDER["v", u]
                act.wait_ge(proj_done, n + 1)
                nc.scalar.activation(v_sb[0:ROWS[u], parity, u * D:u * D + D], bank[0:ROWS[u], PROJ, 0:D],
                                     ACT.Copy).then_inc(proj_free, 1)

            def prepare(b, k, parity):
                for c in SPLIT_AT.get(k, []):
                    if c == 0 and not (isinstance(b, int) and b == 0):
                        act.wait_ge(proj_done, b * PROJ_UNITS)
                    split_hi(b, c)
                for u in K_AT.get(k, []):
                    k_unit(b, u, parity)
                for u in V_AT.get(k, []):
                    v_unit(b, u, parity)

            act.wait_ge(consts_in, CONST_DMAS * 16)
            act.wait_ge(consts_made, CONSTS_MADE)
            with act.Fori(0, TT) as t:
                act.wait_ge(xt_psum, t + 1)
                nc.scalar.activation(xn_t[:, :, :].rearrange("p c n -> p (c n)"), bank[:, 0, 0:D],
                                     ACT.Copy).then_inc(xt_ready, 1)
                act.wait_ge(q_psum, t + 1)
                for g in range(G):
                    nc.scalar.activation(q_tile[:, g, :], bank[:, 1, g * P:g * P + P], ACT.Identity,
                                         bias=bq_scaled[:, g:g + 1], scale=SCALE).then_inc(q_ready, 1)
                act.wait_ge(q_ready, 2 * t + 2)
                nc.scalar.activation(q_hi[:, :, bass.ds(t * P, P)], q_tile[:, :, :], ACT.Copy).then_inc(q_hi_done, 1)
                act.wait_ge(q_split, t + 1)

            for k in range(KT):
                prepare(0, k, 0)

            def tile(t, last):
                for bi in range(2):
                    b = 2 * t + bi
                    for k in range(KT):
                        n = b * KT + k
                        buf = (KT * bi + k) % 2
                        act.wait_ge(scores_done, n + 1)
                        if k >= 2 or bi == 1:
                            act.wait_ge(pv_done, n - 1)
                            act.wait_ge(summed, n - 1)
                        nc.scalar.activation(probs[0:ROWS[k], buf, :].rearrange("p (g n) -> p g n", g=G),
                                             bank[0:ROWS[k], 2 * buf:2 * buf + 2, :], ACT.Exp).then_inc(exp_done, 1)
                        if not (last and bi):
                            prepare(b + 1, k, (bi + 1) % 2)
                act.wait_ge(xn1t_psum, t + 1)
                nc.scalar.activation(xn_t[:, :, :].rearrange("p c n -> p (c n)"), bank[:, 1, 0:D],
                                     ACT.Copy).then_inc(xn1t_ready, 1)
                act.wait_ge(qkv2_psum, t + 1)
                nc.scalar.activation(q_tile[:, :, :], bank[:, 2, 0:G * P].rearrange("p (g n) -> p g n", g=G),
                                     ACT.Copy, scale=SCALE).then_inc(q2_ready, 1)
                nc.scalar.activation(k2_t[:, :, :], bank[:, 2, G * P:2 * G * P].rearrange("p (g n) -> p g n", g=G),
                                     ACT.Copy).then_inc(k2_ready, 1)
                nc.scalar.activation(v2[:, :], bank[:, 3, 0:D], ACT.Copy).then_inc(k2_ready, 1)
                act.wait_ge(st2_psum, t + 1)
                nc.scalar.activation(probs2.rearrange("p (g n) -> p g n", g=G), bank[:, 2:4, :],
                                     ACT.Exp).then_inc(probs2_ready, 1)
                act.wait_ge(xn2t_psum, t + 1)
                nc.scalar.activation(xn_t[:, :, :].rearrange("p c n -> p (c n)"), bank[:, 3, 0:D],
                                     ACT.Copy).then_inc(xn2t_ready, 1)
                act.wait_ge(xn2t_ready, t + 1)
                nc.scalar.activation(xn2_t[:, :, bass.ds(t * P, P)], xn_t[:, :, :], ACT.Copy).then_inc(xn2t_kept, 1)
                act.wait_ge(negmax_ready, t + 1)
                nc.scalar.activation(logits[:, :], bank[:, 0, 0:E], ACT.Exp, bias=row_max[:, :],
                                     accum_out=row_sum[:, :]).then_inc(gexp_ready, 1)
                act.wait_ge(gatest_psum, t + 1)
                nc.scalar.activation(gates_t[:, :], bank[0:E, 1, 0:P], ACT.Copy).then_inc(gatest_ready, 1)

            with act.Fori(0, TT - 1) as t:
                tile(t, False)
            tile(TT - 1, True)

            with act.Fori(0, E // 2) as p:
                for i in range(2):
                    e = 2 * p + i
                    for c in range(HC):
                        act.wait_ge(h_psum, e * HC + c + 1)
                        nc.scalar.activation(h_t[:, c, :], bank[:, c % 4, :], ACT.Gelu,
                                             bias=b1_sb[:, bass.ds(e, 1), c:c + 1].rearrange("p a b -> p (a b)"))\
                            .then_inc(h_ready, 1)

        @block.vector
        def _(dve):
            links = [0]

            def link(ins, base):
                links[0] += 1
                ins.then_inc(dve_step, 1)
                dve.wait_ge(dve_step, base + links[0])

            def layer_norm(src, base, n, done):
                link(nc.vector.bn_stats(stats[:, :], src), base)
                nc.vector.memset(unused[:, :], 0.0)
                link(nc.vector.bn_aggr(mean_var[:, :], stats[:, :]), base)
                nc.vector.tensor_scalar(var_eps[:, :], mean_var[:, 1:2], EPS, None, ALU.add).then_inc(var_ready, 1)
                dve.wait_ge(rstd_ready, n)
                nc.vector.tensor_scalar(xn[:, :], src, mean_var[:, 0:1], rstd[:, :], ALU.subtract,
                                        ALU.mult).then_inc(done, 1)

            def split_lo(b, c):
                dve.wait_ge(ctx_hi_done, b * NC + c + 1)
                nc.vector.tensor_tensor(ctx_lo[:, :, EDGE[c]:EDGE[c + 1]], ctx_raw[:, :, EDGE[c]:EDGE[c + 1]],
                                        ctx_hi[:, :, EDGE[c]:EDGE[c + 1]].bitcast(F32),
                                        ALU.subtract).then_inc(ctx_lo_done, 1)

            def k_unit(b, u, parity):
                c, g = divmod(u, G)
                dve.wait_ge(k_hi_done, b * K_UNITS + u + 1)
                nc.vector.scalar_tensor_tensor(
                    out=k_lo[:, parity, g, EDGE[c]:EDGE[c + 1]], in0=bank[:, PROJ, EDGE[c] - CH[c]:CW], scalar=bias_sb[:, 1, g:g + 1],
                    in1=k_hi[:, parity, g, EDGE[c]:EDGE[c + 1]].bitcast(F32), op0=ALU.add,
                    op1=ALU.subtract).then_inc(proj_free, 1)

            def max_unit(b, u):
                pair, half = divmod(u, HALVES)
                dve.wait_ge(max_psum, b * M_UNITS + u + 1)
                nc.vector.tensor_reduce(maxes[:, pair, half:half + 1], bank[:, SM:SM + 2, 0:CW], AX.XY,
                                        ALU.max).then_inc(max_taken, 1)

            def prepare(b, k, parity, base):
                for c in SPLIT_AT.get(k, []):
                    split_lo(b, c)
                for u in K_AT.get(k, []):
                    k_unit(b, u, parity)
                for u in M_AT.get(k, []):
                    max_unit(b, u)
                if k == KT - 1:
                    dve.wait_ge(max_taken, (b + 1) * M_UNITS)
                    link(nc.vector.tensor_reduce(neg_max[:, :], maxes[:, :, :], AX.X, ALU.max, negate=True), base)
                    nc.vector.tensor_tensor(
                        shift[:, parity], ident[:, :].unsqueeze(1).broadcast_to([P, G * PAIRS, P]),
                        neg_max[:, :].unsqueeze(2).broadcast_to([P, G * PAIRS, P]), ALU.mult).then_inc(shift_ready, 1)

            def finish_heads(ps_o, ps_den, dst, bias, base, done):
                link(nc.vector.reciprocal(recip[:, :], ps_den), base)
                link(nc.vector.tensor_tensor(o_norm[:, :, :, :].rearrange("p g s q -> p (g s q)"), ps_o, recip[:, :],
                                             ALU.mult), base)
                if bias:
                    for g in range(G):
                        ins = nc.vector.tensor_scalar(o_odd[:, g, :], o_norm[:, g, 1, :], mask_sb[:, HG + 1:HG + 2],
                                                      bias_sb[:, 2, g:g + 1], ALU.mult, ALU.add)
                        link(ins, base)
                else:
                    link(nc.vector.tensor_scalar(o_odd[:, :, :], o_norm[:, :, 1, :], mask_sb[:, HG + 1:HG + 2], None,
                                                 ALU.mult), base)
                nc.vector.scalar_tensor_tensor(out=dst, in0=o_norm[:, :, 0, :], scalar=mask_sb[:, HG:HG + 1],
                                               in1=o_odd[:, :, :], op0=ALU.mult, op1=ALU.add).then_inc(done, 1)

            dve.wait_ge(consts_in, CONST_DMAS * 16)
            nc.vector.tensor_copy(ident_bf[:, :], ident[:, :]).then_inc(consts_made, 1)
            nc.vector.tensor_scalar(bq_scaled[:, :], bias_sb[:, 0, :], SCALE, None, ALU.mult).then_inc(consts_made, 1)
            nc.vector.tensor_copy(causal_bf[:, :], causal_sb[:, :]).then_inc(consts_made, 1)
            nc.vector.memset(earlier[:, :, :], 0.0).then_inc(dve_step, 1)
            dve.wait_ge(dve_step, 1)
            for e in range(1, E):
                nc.vector.memset(earlier[:, e, 0:e], 1.0).then_inc(dve_step, 1)
            dve.wait_ge(dve_step, E)
            links[0] = E
            dve.wait_ge(weights_in, 32)
            for w, hi, lo in ((0, wk_hi, wk_lo), (1, wv_hi, wv_lo)):
                link(nc.vector.tensor_copy(hi[:, :, :], w_raw[:, w]), 0)
                nc.vector.tensor_tensor(lo[:, :, :], w_raw[:, w], hi[:, :, :].bitcast(F32),
                                        ALU.subtract).then_inc(raw_split, 1)
            start = links[0]

            dve.wait_ge(x_in, 16)
            LN_LINKS = 2
            with dve.Fori(0, TT) as t:
                links[0] = start
                base = t * LN_LINKS
                layer_norm(x_all[:, bass.ds(t, 1), :].rearrange("p a n -> p (a n)"), base, t + 1, xn_ready)
                assert links[0] == start + LN_LINKS
                dve.wait_ge(q_hi_done, t + 1)
                nc.vector.tensor_tensor(q_lo[:, :, bass.ds(t * P, P)], q_tile[:, :, :],
                                        q_hi[:, :, bass.ds(t * P, P)].bitcast(F32), ALU.subtract).then_inc(q_split, 1)
            links[0] = start = start + TT * LN_LINKS
            for k in range(KT):
                prepare(0, k, 0, 0)
            start = links[0]

            def batch(t, bi, last, base):
                b = 2 * t + bi
                for k in range(KT):
                    if not (last and bi):
                        prepare(b + 1, k, (bi + 1) % 2, base)
                dve.wait_ge(denom_done, b + 1)
                finish_heads(bank[:, O, 0:2 * P], bank[:, O, 2 * P:4 * P], o_t[:, :, bi * Q:bi * Q + Q], True, base,
                             o_ready)

            def tile(t, last, base):
                links[0] = start
                for bi in range(2):
                    batch(t, bi, last, base)
                dve.wait_ge(y1_psum, t + 1)
                x_tile = x_all[:, bass.ds(t, 1), :].rearrange("p a n -> p (a n)")
                link(nc.vector.tensor_tensor(x1[:, :], bank[:, 0, 0:D], x_tile, ALU.add), base)
                layer_norm(x1[:, :], base, TT + 2 * t + 1, xn1_ready)
                dve.wait_ge(q2_ready, t + 1)
                for bi in range(2):
                    nc.vector.tensor_tensor(
                        qbd2[:, bi], q_tile[:, :, bi * Q:bi * Q + Q].unsqueeze(2).broadcast_to([P, G, HG, Q]),
                        mask_sb[:, 0:HG].unsqueeze(1).unsqueeze(3).broadcast_to([P, G, HG, Q]),
                        ALU.mult).then_inc(qbd2_ready, 1)
                for bi in range(2):
                    dve.wait_ge(s2_psum, 2 * t + bi + 1)
                    link(nc.vector.tensor_tensor(masked[:, bi], bank[:, bi, :].rearrange("p (n k) -> p n k", k=Q),
                                                 causal_sb[:, :].unsqueeze(1).broadcast_to([P, G * PAIRS, Q]),
                                                 ALU.add), base)
                    link(nc.vector.tensor_reduce(neg_max[:, :], masked[:, bi], AX.X, ALU.max, negate=True), base)
                    nc.vector.tensor_tensor(
                        shift2[:, bi], ident[:, :].unsqueeze(1).broadcast_to([P, G * PAIRS, P]),
                        neg_max[:, :].unsqueeze(2).broadcast_to([P, G * PAIRS, P]), ALU.mult).then_inc(shift2_ready, 1)
                for bi in range(2):
                    dve.wait_ge(o2_psum, 2 * t + bi + 1)
                    finish_heads(bank[:, bi, 0:2 * P], bank[:, bi, 2 * P:4 * P], o2_t[:, :, bi * Q:bi * Q + Q], False,
                                 base, o2_ready)
                dve.wait_ge(y2_psum, t + 1)
                link(nc.vector.tensor_tensor(x1[:, :], bank[:, 2, 0:D], x1[:, :], ALU.add), base)
                layer_norm(x1[:, :], base, TT + 2 * t + 2, xn2_ready)
                dve.wait_ge(logits_psum, t + 1)
                nc.vector.tensor_reduce(row_max[:, :], bank[:, 0, 0:E], AX.X, ALU.max, negate=True)\
                    .then_inc(negmax_ready, 1)
                dve.wait_ge(gexp_ready, t + 1)
                link(nc.vector.reciprocal(row_sum[:, :], row_sum[:, :]), base)
                link(nc.vector.tensor_scalar(logits[:, :], logits[:, :], row_sum[:, :], None, ALU.mult), base)
                mine = logits[:, :].unsqueeze(2).broadcast_to([P, E, E])
                other = logits[:, :].unsqueeze(1).broadcast_to([P, E, E])
                link(nc.vector.tensor_tensor(above[:, :, :], other, mine, ALU.is_gt), base)
                link(nc.vector.tensor_tensor(ties[:, :, :], other, mine, ALU.is_equal), base)
                link(nc.vector.tensor_tensor(ties[:, :, :], ties[:, :, :], earlier[:, :, :], ALU.mult), base)
                link(nc.vector.tensor_tensor(above[:, :, :], above[:, :, :], ties[:, :, :], ALU.add), base)
                link(nc.vector.tensor_reduce(rank[:, :], above[:, :, :], AX.X, ALU.add), base)
                nc.vector.scalar_tensor_tensor(out=gate_tile[:, :], in0=rank[:, :], scalar=1.5, in1=logits[:, :],
                                               op0=ALU.is_lt, op1=ALU.mult).then_inc(gates_ready, 1)
                dve.wait_ge(gates_ready, t + 1)
                nc.vector.tensor_copy(gates[:, bass.ds(t, 1), :].rearrange("p a n -> p (a n)"), gate_tile[:, :])
                dve.wait_ge(bias2_psum, t + 1)
                nc.vector.tensor_tensor(x_tile, x1[:, :], bank[:, 2, 0:D], ALU.add).then_inc(tile_done, 1)

            with dve.Fori(0, TT - 1) as t:
                tile(t, False, t * TILE_LINKS)
                assert links[0] - start == TILE_LINKS, links[0] - start
            tile(TT - 1, True, (TT - 1) * TILE_LINKS)

            with dve.Fori(0, E // 2) as p:
                for i in range(2):
                    e = 2 * p + i
                    dve.wait_ge(y_psum, e + 1)
                    for t in range(TT):
                        ins = nc.vector.scalar_tensor_tensor(
                            out=x_all[:, t, :], in0=bank[:, 4 + t // 2, (t % 2) * D:(t % 2) * D + D],
                            scalar=gates[:, t, bass.ds(e, 1)], in1=x_all[:, t, :],
                            op0=ALU.mult, op1=ALU.add)
                    ins.then_inc(y_taken, 1)

        @block.tensor
        def _(pe):
            def split_product(dst, pairs):
                n = 0
                for (a_hi, a_lo), (b_hi, b_lo) in pairs:
                    for lhs, rhs in ((a_hi, b_hi), (a_hi, b_lo), (a_lo, b_hi)):
                        n += 1
                        last = nc.tensor.matmul(dst, lhs, rhs, start=(n == 1), stop=(n == 3 * len(pairs)))
                return last

            def wait_proj(b, n):
                if isinstance(b, int) and b == 0 and n == 0:
                    return
                pe.wait_ge(proj_free, b * PROJ_UNITS + n)

            def k_unit(b, u):
                n = ORDER["k", u]
                c, g = divmod(u, G)
                wait_proj(b, n)
                if g == 0:
                    pe.wait_ge(ctx_lo_done, b * NC + c + 1)
                cols, keys = slice(g * P, g * P + P), slice(CH[c], CH[c] + CW)
                split_product(bank[:, PROJ, 0:CW],
                              [((wk_hi[:, d, cols], wk_lo[:, d, cols]), (ctx_hi[:, d, keys], ctx_lo[:, d, keys]))
                               for d in range(DC)]).then_inc(proj_done, 1)

            def v_unit(b, u):
                n = ORDER["v", u]
                wait_proj(b, n)
                keys = slice(u * P, u * P + ROWS[u])
                c = next(c for c in range(NC) if EDGE[c + 1] >= keys.stop)
                pe.wait_ge(ctx_lo_done, b * NC + c + 1)
                split_product(bank[0:ROWS[u], PROJ, 0:D],
                              [((ctx_hi[:, d, keys], ctx_lo[:, d, keys]), (wv_hi[:, d, :], wv_lo[:, d, :]))
                               for d in range(DC)]).then_inc(proj_done, 1)

            def max_unit(b, u, parity):
                pair, half = divmod(u, HALVES)
                g, j = divmod(pair, PAIRS)
                if not (isinstance(b, int) and b == 0 and u == 0):
                    pe.wait_ge(max_taken, b * M_UNITS + u)
                if u == 0:
                    pe.wait_ge(proj_free, b * PROJ_UNITS + ORDER["k", K_UNITS - 1] + 1)
                    pe.wait_ge(qbd_ready, 2 * (b + 1))
                for i in range(2):
                    c = 2 * half + i
                    ins = nc.tensor.matmul(bank[:, SM + i, 0:CW],
                                           qbd_hi[:, parity, g, 2 * j:2 * j + 2, :].rearrange("p s q -> p (s q)"),
                                           k_hi[:, parity, g, CH[c]:CH[c] + CW], start=True, stop=True)
                ins.then_inc(max_psum, 1)

            def prepare(b, k, parity):
                for u in K_AT.get(k, []):
                    k_unit(b, u)
                for u in M_AT.get(k, []):
                    max_unit(b, u, parity)
                for u in V_AT.get(k, []):
                    v_unit(b, u)

            def scores(b, bi, k):
                n = b * KT + k
                rows, buf = ROWS[k], (KT * bi + k) % 2
                if k >= 2 or bi == 1:
                    pe.wait_ge(exp_done, n - 1)
                if k == 0:
                    pe.wait_ge(shift_ready, b + 1)
                keys = slice(k * P, k * P + rows)
                for g in range(G):
                    dst = bank[0:rows, 2 * buf + g, :]
                    hi = qbd_hi[:, bi, g].rearrange("p h q -> p (h q)")
                    lo = qbd_lo[:, bi, g].rearrange("p h q -> p (h q)")
                    nc.tensor.matmul(dst, k_hi[:, bi, g, keys], hi, start=True, stop=False)
                    nc.tensor.matmul(dst, k_hi[:, bi, g, keys], lo, start=False, stop=False)
                    nc.tensor.matmul(dst, k_lo[:, bi, g, keys], hi, start=False, stop=False)
                    ins = nc.tensor.matmul(dst, ones_bf[:, 0:rows],
                                           shift[:, bi, g * PAIRS:(g + 1) * PAIRS].rearrange("p j c -> p (j c)"),
                                           start=False, stop=True)
                ins.then_inc(scores_done, 1)

            def weigh(b, bi, k):
                n = b * KT + k
                rows, buf = ROWS[k], (KT * bi + k) % 2
                pe.wait_ge(exp_done, n + 1)
                if k == 0 and (bi == 1 or not isinstance(b, int) or b > 0):
                    if bi == 1:
                        pe.wait_ge(o_ready, b)
                for g in range(G):
                    for j in range(PAIRS):
                        v_at = k * D + g * P + 32 * j
                        ins = nc.tensor.matmul(bank[32 * j:32 * j + 32, O, g * P:g * P + P],
                                               v_sb[0:rows, bi, v_at:v_at + 32],
                                               probs[0:rows, buf, (g * PAIRS + j) * P:(g * PAIRS + j + 1) * P],
                                               start=(k == 0 and g == 0), stop=(k == KT - 1), skip_group_check=True)
                ins.then_inc(pv_done, 1)

            def denominators(b):
                pe.wait_ge(summed, (b + 1) * KT)
                for g in range(G):
                    for j in range(PAIRS):
                        ins = nc.tensor.matmul(bank[32 * j:32 * j + 32, O, (G + g) * P:(G + g + 1) * P], ones_f[:, 0:32],
                                               prob_sum[:, (g * PAIRS + j) * P:(g * PAIRS + j + 1) * P],
                                               start=False, stop=True, skip_group_check=True)
                ins.then_inc(denom_done, 1)

            def transposes(dst):
                for c in range(DC):
                    ins = nc.tensor.transpose(dst[:, c * P:c * P + P], xn[:, c * P:c * P + P], ident[:, :])
                return ins

            pe.wait_ge(consts_in, CONST_DMAS * 16)
            pe.wait_ge(consts_made, CONSTS_MADE)
            pe.wait_ge(weights_in, 32)
            with pe.Fori(0, TT) as t:
                pe.wait_ge(xn_ready, t + 1)
                transposes(bank[:, 0, :]).then_inc(xt_psum, 1)
                pe.wait_ge(xt_ready, t + 1)
                for g in range(G):
                    for c in range(DC):
                        ins = nc.tensor.matmul(bank[:, 1, g * P:g * P + P], w_sb[:, 0, c, g * P:g * P + P],
                                               xn_t[:, c, :], start=(c == 0), stop=(c == DC - 1))
                ins.then_inc(q_psum, 1)
            pe.wait_ge(q_split, TT)
            pe.wait_ge(raw_split, 2)
            for k in range(KT):
                prepare(0, k, 0)

            def tile(t, last):
                for bi in range(2):
                    b = 2 * t + bi
                    for k in range(KT):
                        scores(b, bi, k)
                        if not (last and bi):
                            prepare(b + 1, k, (bi + 1) % 2)
                        if k:
                            weigh(b, bi, k - 1)
                    weigh(b, bi, KT - 1)
                    denominators(b)
                pe.wait_ge(o_ready, 2 * t + 2)
                for g in range(G):
                    nc.tensor.matmul(bank[:, 0, 0:D], o_t[:, g, :], w_sb[:, 1, g, :], start=(g == 0), stop=False)
                nc.tensor.matmul(bank[:, 0, 0:D], ones_f[0:1, :], bo_sb[:, :], start=False, stop=True)\
                    .then_inc(y1_psum, 1)
                pe.wait_ge(xn1_ready, t + 1)
                transposes(bank[:, 1, :]).then_inc(xn1t_psum, 1)
                pe.wait_ge(xn1t_ready, t + 1)
                for w in range(2):
                    for g in range(G):
                        for c in range(DC):
                            nc.tensor.matmul(bank[:, 2, (w * G + g) * P:(w * G + g + 1) * P],
                                             w_sb[:, 2 + w, c, g * P:g * P + P], xn_t[:, c, :],
                                             start=(c == 0), stop=(c == DC - 1))
                for c in range(DC):
                    ins = nc.tensor.matmul(bank[:, 3, 0:D], xn_t[:, c, :], w_sb[:, 4, c, :], start=(c == 0),
                                           stop=(c == DC - 1))
                ins.then_inc(qkv2_psum, 1)
                pe.wait_ge(qbd2_ready, 2 * (t + 1))
                pe.wait_ge(k2_ready, 2 * (t + 1))
                for bi in range(2):
                    for g in range(G):
                        for j in range(PAIRS):
                            n = g * PAIRS + j
                            ins = nc.tensor.matmul(bank[:, bi, n * Q:n * Q + Q],
                                                   qbd2[:, bi, g, 2 * j:2 * j + 2, :].rearrange("p s q -> p (s q)"),
                                                   k2_t[:, g, bi * Q:bi * Q + Q], start=True, stop=True)
                    ins.then_inc(s2_psum, 1)
                for bi in range(2):
                    pe.wait_ge(shift2_ready, 2 * t + bi + 1)
                    for g in range(G):
                        dst = bank[bi * Q:bi * Q + Q, 2 + g, :]
                        nc.tensor.matmul(dst, k2_t[:, g, bi * Q:bi * Q + Q], qbd2[:, bi, g].rearrange("p h q -> p (h q)"),
                                         start=True, stop=False)
                        nc.tensor.matmul(dst, ones_bf[:, 0:Q],
                                         shift2[:, bi, g * PAIRS:(g + 1) * PAIRS].rearrange("p j c -> p (j c)"),
                                         start=False, stop=False)
                        ins = nc.tensor.matmul(dst, causal_bf[:, :],
                                               ident_bf[:, :].unsqueeze(1).broadcast_to([P, PAIRS, P]),
                                               start=False, stop=True)
                ins.then_inc(st2_psum, 1)
                pe.wait_ge(consts_made, CONSTS_MADE)
                pe.wait_ge(probs2_ready, t + 1)
                for bi in range(2):
                    rows = slice(bi * Q, bi * Q + Q)
                    for what in range(2):
                        for g in range(G):
                            for j in range(PAIRS):
                                lhs = ones_f[rows, 0:32] if what else v2[rows, g * P + 32 * j:g * P + 32 * j + 32]
                                ins = nc.tensor.matmul(
                                    bank[32 * j:32 * j + 32, bi, (what * G + g) * P:(what * G + g + 1) * P], lhs,
                                    probs2[rows, (g * PAIRS + j) * P:(g * PAIRS + j + 1) * P],
                                    start=(what == 0 and g == 0), stop=True, skip_group_check=True)
                    ins.then_inc(o2_psum, 1)
                pe.wait_ge(o2_ready, 2 * (t + 1))
                for g in range(G):
                    ins = nc.tensor.matmul(bank[:, 2, 0:D], o2_t[:, g, :], w_sb[:, 5, g, :], start=(g == 0),
                                           stop=(g == G - 1))
                ins.then_inc(y2_psum, 1)
                pe.wait_ge(xn2_ready, t + 1)
                transposes(bank[:, 3, :]).then_inc(xn2t_psum, 1)
                pe.wait_ge(xn2t_ready, t + 1)
                for c in range(DC):
                    nc.tensor.matmul(bank[:, 0, 0:E], xn_t[:, c, :], wg_sb[:, c, :], start=(c == 0), stop=False)
                nc.tensor.matmul(bank[:, 0, 0:E], ones_f[0:1, :], bg_sb[:, :], start=False, stop=True)\
                    .then_inc(logits_psum, 1)
                pe.wait_ge(gates_ready, t + 1)
                nc.tensor.transpose(bank[0:E, 1, 0:P], gate_tile[:, :], ident[:, :]).then_inc(gatest_psum, 1)
                pe.wait_ge(gatest_ready, t + 1)
                nc.tensor.matmul(bank[:, 2, 0:D], gates_t[:, :], b2_sb[:, :], start=True, stop=True)\
                    .then_inc(bias2_psum, 1)
                pe.wait_ge(tile_done, t + 1)

            with pe.Fori(0, TT - 1) as t:
                tile(t, False)
            tile(TT - 1, True)
            pe.wait_ge(xn2t_kept, TT)

            with pe.Fori(0, E // 2) as p:
                for i in range(2):
                    e = 2 * p + i
                    pe.wait_ge(w_in[i], 32 * (p + 1))
                    for c in range(HC + 1):
                        if c < HC:
                            if c >= 4 or i == 1:
                                pe.wait_ge(h_ready, e * HC + c - 3)
                            for d in range(DC):
                                ins = nc.tensor.matmul(bank[:, c % 4, :], w1_sb[i][:, d, c * P:c * P + P],
                                                       xn2_t[:, d, :], start=(d == 0), stop=(d == DC - 1))
                            ins.then_inc(h_psum, 1)
                        if c:
                            pe.wait_ge(h_ready, e * HC + c)
                            if c == 1 and i == 1:
                                pe.wait_ge(y_taken, e)
                            for t in range(TT):
                                ins = nc.tensor.matmul(bank[:, 4 + t // 2, (t % 2) * D:(t % 2) * D + D],
                                                       h_t[:, c - 1, t * P:t * P + P], w2_sb[i][:, c - 1, :],
                                                       start=(c == 1 and t % 2 == 0), stop=(c == HC),
                                                       skip_group_check=True)
                    ins.then_inc(y_psum, 1)
                pe.wait_ge(y_taken, 2 * p + 2)


def kernel(**a):
    import numpy as np
    import concourse.bacc as bacc
    from concourse.bass_utils import run_bass_kernel_spmd

    def t(w):
        w = np.asarray(w)
        return w.T.reshape(DC, P, -1).transpose(1, 0, 2)

    f = {k: np.asarray(v) for k, v in a.items()}
    wi = f["L0_attn_in_proj_weight"]
    ctx = f["ctx_1024"].transpose(0, 2, 1).reshape(B, DC, P, S).transpose(0, 2, 1, 3)
    weights = np.stack([t(f["L0_xattn_Wq"]), t(f["L0_xattn_Wo"]), t(wi[0:D]), t(wi[D:2 * D]), t(wi[2 * D:3 * D]),
                        t(f["L0_attn_out_proj_weight"]), t(f["L0_xattn_Wk"]), t(f["L0_xattn_Wv"])], 1)
    biases = np.stack([f["L0_xattn_" + n].reshape(DC, P).T for n in ("bq", "bk", "bv")], 1)
    row = np.arange(P)
    head = (row[:, None] // DK == np.arange(HG)[None]).astype(np.float32)
    parity = (row[:, None] // DK % 2 == np.arange(2)[None]).astype(np.float32)
    hidden = np.where(np.arange(Q)[None] > (row % Q)[:, None], np.float32(FAR), np.float32(0))
    arrays = {
        "x": f["x"].reshape(TT, P, D).transpose(1, 0, 2),
        "ctx_t": ctx, "w_t": weights, "wg_t": t(f["L0_ffn_Wg"].T), "biases": biases,
        "bo_row": f["L0_xattn_bo"][None], "bg_row": f["L0_ffn_bg"][None],
        "w1": f["L0_ffn_W1"].reshape(E, DC, P, HID).transpose(0, 2, 1, 3),
        "b1": f["L0_ffn_b1"].reshape(E, HC, P).transpose(2, 0, 1),
        "w2": f["L0_ffn_W2"].reshape(E, HC, P, D).transpose(0, 2, 1, 3),
        "b2": f["L0_ffn_b2"],
        "eye": np.eye(P, dtype=np.float32), "masks": np.concatenate([head, parity], 1), "causal": hidden,
    }
    nc = bacc.Bacc("TRN2", target_bir_lowering=False, num_devices=1)
    args, feeds = [], {}
    for name, v in arrays.items():
        v = np.ascontiguousarray(v)
        feeds["in_" + name] = v
        args.append(nc.dram_tensor("in_" + name, v.shape, mybir.dt.from_np(v.dtype), kind="ExternalInput").ap())
    out = nc.dram_tensor("result", (P, TT, D), F32, kind="ExternalOutput").ap()
    perceiver_kernel(nc, *args, out)
    r = run_bass_kernel_spmd(nc, [feeds], core_ids=[0])
    return r.results[0]["result"].transpose(1, 0, 2).reshape(B, Q, D)
```

```python
from contextlib import ExitStack

import concourse.bass as bass
from concourse import mybir

F32 = mybir.dt.float32
F32R = mybir.dt.float32r
BF16 = mybir.dt.bfloat16
ACT = mybir.ActivationFunctionType
ALU = mybir.AluOpType
AX = mybir.AxisListType

P = 128
B, Q, D = 8, 64, 256
S = 1601
H, DK = 16, 16
DC = D // P
HG = P // DK
G = H // HG
PAIRS = HG // 2
TOK = B * Q
TT = TOK // P
KT = -(-S // P)
ROWS = [min(P, S - P * k) for k in range(KT)]
CW = 402
CH = [0, 400, 800, S - CW]
NC = len(CH)
EDGE = [0] + [c + CW for c in CH]
E, HID = 8, 1024
HC = HID // P
EPS = 1e-5
SCALE = 0.25
FAR = -1e30


STEPS = 2 * KT
CONST_DMAS = 8
CONSTS_MADE = 5
RING = 3
TILE_LINKS = 25
K_UNITS = G * NC
PIECES = 4
PIECE = DC * HID // PIECES

SPLIT_AT = {0: [0, 1], 1: [2], 2: [3]}
K_AT = {1: [0, 1], 2: [2, 3], 3: [4, 5], 4: [6, 7]}
V_AT = {k: [k - 1] for k in range(1, KT - 1)} | {KT - 1: [KT - 2, KT - 1]}
M_AT = {5: range(0, 5), 6: range(5, 10), 7: range(10, 15), 8: range(15, 20), 9: range(20, 24), 10: range(24, 28),
        11: range(28, 32)}
CHAIN_AT = {3: ["y1"], 5: ["xt1"], 6: ["qk", "v"], 8: ["s0"], 10: ["st00", "st01"], 12: ["s1"], 14: ["st10", "st11"],
            15: ["o0"], 16: ["o1"], 18: ["y2"], 20: ["xt2"], 21: ["router"], 23: ["gt"], 24: ["b2"]}
SPLIT_W_AT = [10, 12, 14, 15, 16, 18, 20, 21]
READ_BY_ACT = {"v", "V", "xt1", "qk", "st00", "st01", "st10", "st11", "xt2", "router", "gt"}


class Units:

    def __init__(self, before, batch_after, chain, spare=0):
        self.before = before
        self.at = {}
        order = []
        for s in range(STEPS):
            bi, k = divmod(s, KT)
            row = []
            if batch_after > bi:
                row += [("K", u) for u in K_AT.get(k, [])] + [("M", u) for u in M_AT.get(k, [])]
            if chain:
                row += [(c, 0) for c in CHAIN_AT.get(s, [])]
            if batch_after > bi:
                row += [("V", u) for u in V_AT.get(k, [])]
            self.at[s] = []
            for kind, u in row:
                self.at[s].append((len(order), kind, u))
                order.append(kind)
        self.by_act = [k in READ_BY_ACT for k in order]

    def counts(self, n):
        a = sum(self.by_act[:n])
        return n, a, n - a

    def total(self):
        return self.counts(len(self.by_act))

    def wait_filled(self, eng, sem, n):
        eng.wait_ge(sem, self.before[0] + n + 1)

    def wait_read_act(self, eng, by_act, kind):
        n = next(n for s in range(STEPS) for n, k, _ in self.at[s] if k == kind)
        eng.wait_ge(by_act, self.before[1] + self.counts(n + 1)[1])

    def wait_free(self, eng, by_act, by_dve, n):
        if n < RING:
            if n == 0 and not (isinstance(self.before[1], int) and self.before[1] == 0):
                eng.wait_ge(by_act, self.before[1])
                eng.wait_ge(by_dve, self.before[2])
            return
        a, d = self.counts(n - RING + 1)[1:]
        if self.by_act[n - RING]:
            eng.wait_ge(by_act, self.before[1] + a)
        else:
            eng.wait_ge(by_dve, self.before[2] + d)


def add(a, b, times=1):
    return tuple(x + times * y for x, y in zip(a, b))


def runs():
    prologue = Units((0, 0, 0), 0, False)
    order = []
    for s in range(KT):
        row = [("K", u) for u in K_AT.get(s, [])] + [("M", u) for u in M_AT.get(s, [])]
        row += [("V", u) for u in V_AT.get(s, [])]
        prologue.at[s] = [(len(order) + i, *r) for i, r in enumerate(row)]
        order += [kind for kind, _ in row]
    prologue.by_act = [k in READ_BY_ACT for k in order]
    first = Units(prologue.total(), 2, False)
    start = add(first.before, first.total())
    middle_total = Units(start, 2, True).total()

    def middle(t):
        return Units(add(start, middle_total, t - 1), 2, True)

    last = Units(add(start, middle_total, TT - 2), 1, True)
    tail = Units(add(last.before, last.total()), 0, True)
    return prologue, first, middle, last, tail


PROLOGUE, FIRST, MIDDLE, LAST, TAIL = runs()


def perceiver_kernel(nc, x, ctx_t, w_t, wg_t, biases, bo_row, bg_row, w1, b1, w2, b2, eye, masks, causal, out):
    stack = ExitStack()
    with stack:
        def sem(name):
            return stack.enter_context(nc.semaphore(name))

        def sb(name, shape, dt=F32, where=stack):
            return where.enter_context(nc.sbuf_tensor(name, shape, dt))

        ident = sb("ident", [P, P])
        ones_bf = sb("ones_bf", [P, P], BF16)
        ident_bf = sb("ident_bf", [P, P], BF16)
        ones_f = sb("ones_f", [P, P])
        zero = sb("zero", [P, 1])
        neg_half = sb("neg_half", [P, TT])
        unused = sb("unused", [P, 1])
        mask_sb = sb("mask_sb", [P, HG + 2])
        bias_sb = sb("bias_sb", [P, 3, DC])
        bq_scaled = sb("bq_scaled", [P, DC])
        bo_sb = sb("bo_sb", [1, D])
        bo_all = sb("bo_all", [1, D])
        bg_sb = sb("bg_sb", [1, E])
        wg_sb = sb("wg_sb", [P, DC, E])
        b1_sb = sb("b1_sb", [P, E, HC])
        b2_sb = sb("b2_sb", [E, D])
        x_all = sb("x_all", [P, TT, D])
        xn2_hi = sb("xn2_hi", [P, DC, TOK], F32R)
        xn2_lo = sb("xn2_lo", [P, DC, TOK], F32R)
        gates = sb("gates", [P, TT, E])
        w_sb = sb("w_sb", [P, 6, DC, D])
        causal_sb = sb("causal_sb", [P, Q])
        causal_bf = sb("causal_bf", [P, Q], BF16)
        o_t = sb("o_t", [P, G, P])
        stats = sb("stats", [P, TT, 6])
        mean_var = sb("mean_var", [P, TT, 2])
        var_eps = sb("var_eps", [P, TT])
        rstd = sb("rstd", [P, TT])
        x1 = sb("x1", [P, D])
        xn = sb("xn", [P, D])
        xn_t = sb("xn_t", [P, DC, P])
        q2_t = sb("q2_t", [P, G, P])
        k2_t = sb("k2_t", [P, G, P])
        v2 = sb("v2", [P, D])
        qbd2 = sb("qbd2", [P, G, HG, Q])
        masked = sb("masked", [P, G * PAIRS, Q])
        own = masked[:, 0:2 * G, :]
        odd = masked[:, 2 * G:4 * G, :]
        neg_max2 = sb("neg_max2", [P, G * PAIRS])
        shift2 = sb("shift2", [P, G * PAIRS, P], BF16)
        probs2 = sb("probs2", [P, G * 512])
        o2_t = sb("o2_t", [P, G, P])
        logits = sb("logits", [P, E])
        row_max = sb("row_max", [P, 1])
        row_sum = sb("row_sum", [P, 1])
        above = sb("above", [P, E, E])
        ties = sb("ties", [P, E, E])
        rank = sb("rank", [P, E])
        earlier = sb("earlier", [P, E, E])
        gate_tile = sb("gate_tile", [P, E])
        gates_t = sb("gates_t", [E, P])

        attn = ExitStack()
        with attn:
            wk_hi = sb("wk_hi", [P, DC, D], F32R, attn)
            wk_lo = sb("wk_lo", [P, DC, D], F32R, attn)
            wv_hi = sb("wv_hi", [P, DC, D], F32R, attn)
            wv_lo = sb("wv_lo", [P, DC, D], F32R, attn)
            q_hi = sb("q_hi", [P, G, TOK], F32R, attn)
            q_lo = sb("q_lo", [P, G, TOK], F32R, attn)
            ctx_raw = sb("ctx_raw", [P, 2, DC, CW], F32, attn)
            ctx_hi = sb("ctx_hi", [P, DC, S], F32R, attn)
            ctx_lo = sb("ctx_lo", [P, DC, S], F32R, attn)
            k_hi = sb("k_hi", [P, 2, G, S], F32R, attn)
            k_lo = sb("k_lo", [P, 2, G, S], F32R, attn)
            v_sb = sb("v_sb", [P, 2, KT * D], F32, attn)
            probs = sb("probs", [P, 2, G * 512], F32, attn)
            prob_sum = sb("prob_sum", [P, G * 512], F32, attn)
            qbd_hi = sb("qbd_hi", [P, 2, G, HG, Q], F32R, attn)
            qbd_lo = sb("qbd_lo", [P, 2, G, HG, Q], F32R, attn)
            maxes = sb("maxes", [P, G * PAIRS, NC], F32, attn)
            neg_max = sb("neg_max", [P, G * PAIRS], F32, attn)
            shift = sb("shift", [P, 2, G * PAIRS, P], BF16, attn)
        xn_all = v_sb[:, 1, 0:TT * D].rearrange("p (t n) -> p t n", t=TT)
        xn_all_t = v_sb[:, 1, TT * D:2 * TT * D].rearrange("p (c n) -> p c n", c=DC)
        q_all = v_sb[:, 1, 2 * TT * D:3 * TT * D].rearrange("p (g n) -> p g n", g=G)
        w_raw = probs[:, 0, :].rearrange("p (w c n) -> p w c n", w=2, c=DC)

        moe = ExitStack()
        with moe:
            raw_sb = [sb(f"raw_sb{i}", [P, 2, DC * HID], F32, moe) for i in range(2)]
            w_hi = [sb(f"w_hi{i}", [P, 2, DC * HID], F32R, moe) for i in range(2)]
            w_lo = [sb(f"w_lo{i}", [P, 2, DC * HID], F32R, moe) for i in range(2)]
            h_raw = sb("h_raw", [P, 2, TOK], F32, moe)
            h_hi = sb("h_hi", [P, 4, TOK], F32R, moe)
            h_lo = sb("h_lo", [P, 4, TOK], F32R, moe)

        bank = stack.enter_context(nc.psum_tensor("bank", [P, 8, 512], F32))
        UNIT, O = 4, 7

        consts_in = sem("consts_in")
        kv_weights_in = sem("kv_weights_in")
        weights_in = sem("weights_in")
        x_in = sem("x_in")
        ctx_in = [sem(f"ctx_in{i}") for i in range(2)]
        consts_made = sem("consts_made")
        exponent_made = sem("exponent_made")
        kv_weights_split = sem("kv_weights_split")
        stats_ready = sem("stats_ready")
        rstd_ready = sem("rstd_ready")
        xn_ready = sem("xn_ready")
        xt_psum = sem("xt_psum")
        xt_ready = sem("xt_ready")
        q_psum = sem("q_psum")
        q_ready = sem("q_ready")
        q_hi_done = sem("q_hi_done")
        q_split = sem("q_split")
        bo_psum = sem("bo_psum")
        qbd_ready = sem("qbd_ready")
        ctx_hi_done = sem("ctx_hi_done")
        ctx_lo_done = sem("ctx_lo_done")
        filled = sem("filled")
        read_act = sem("read_act")
        read_dve = sem("read_dve")
        k_hi_done = sem("k_hi_done")
        shift_ready = sem("shift_ready")
        scores_done = sem("scores_done")
        exp_done = sem("exp_done")
        pv_done = sem("pv_done")
        summed = sem("summed")
        denom_done = sem("denom_done")
        o_ready = sem("o_ready")
        dve_step = sem("dve_step")
        xn1_ready = sem("xn1_ready")
        qbd2_ready = sem("qbd2_ready")
        shift2_ready = sem("shift2_ready")
        o2_ready = sem("o2_ready")
        xn2_ready = sem("xn2_ready")
        xn2_hi_done = sem("xn2_hi_done")
        negmax_ready = sem("negmax_ready")
        gates_ready = sem("gates_ready")
        tile_done = sem("tile_done")
        w_in = [sem(f"w_in{i}") for i in range(2)]
        w_hi_done = sem("w_hi_done")
        w_split = sem("w_split")
        h_psum = sem("h_psum")
        h_ready = sem("h_ready")
        h_split = sem("h_split")
        y_chunk = sem("y_chunk")
        y_taken = sem("y_taken")
        stored = sem("stored")

        block = stack.enter_context(nc.Block())

        def is_first(b):
            return isinstance(b, int) and b == 0

        @block.sync
        def _(sp):
            sp.dma_start(x_all[:, :, :], x).then_inc(x_in, 16)

            def load(b, c):
                sp.dma_start(ctx_raw[:, c % 2, :, 0:EDGE[c + 1] - EDGE[c]],
                             ctx_t[b, :, :, EDGE[c]:EDGE[c + 1]]).then_inc(ctx_in[c % 2], 16)

            sp.dma_start(w_raw, w_t[:, 6:8]).then_inc(kv_weights_in, 16)
            load(0, 0)
            load(0, 1)
            for dst, src in ((ident[:, :], eye), (bias_sb[:, :, :], biases), (bo_sb[:, :], bo_row),
                             (bg_sb[:, :], bg_row), (wg_sb[:, :, :], wg_t),
                             (b1_sb[:, :, :], b1), (b2_sb[:, :], b2), (causal_sb[:, :], causal)):
                sp.dma_start(dst, src).then_inc(consts_in, 16)
            for c in range(2, NC):
                sp.wait_ge(ctx_lo_done, c - 1)
                load(0, c)
            with sp.Fori(1, B) as b:
                for c in range(NC):
                    sp.wait_ge(ctx_lo_done, b * NC + c - 1)
                    load(b, c)
            sp.wait_ge(denom_done, B)
            for e in range(2):
                sp.dma_start(raw_sb[e][:, 0], w1[e]).then_inc(w_in[e], 16)
                sp.dma_start(raw_sb[e][:, 1], w2[e]).then_inc(w_in[e], 16)
            with sp.Fori(1, E // 2) as p:
                for i in range(2):
                    sp.wait_ge(w_split, (2 * p + i - 1) * 2 * PIECES)
                    sp.dma_start(raw_sb[i][:, 0], w1[2 * p + i]).then_inc(w_in[i], 16)
                    sp.dma_start(raw_sb[i][:, 1], w2[2 * p + i]).then_inc(w_in[i], 16)
            sp.wait_ge(y_taken, E)
            sp.dma_start(out, x_all[:, :, :]).then_inc(stored, 16)
            sp.wait_ge(stored, 16)

        @block.gpsimd
        def _(pool):
            nc.gpsimd.memset(zero[:, :], 0.0).then_inc(consts_made, 1)
            nc.gpsimd.memset(neg_half[:, :], -0.5).then_inc(exponent_made, 1)
            nc.gpsimd.memset(ones_bf[:, :], 1.0).then_inc(consts_made, 1)
            nc.gpsimd.memset(ones_f[:, :], 1.0).then_inc(consts_made, 1)
            pool.dma_start(mask_sb[:, :], masks).then_inc(weights_in, 16)
            pool.dma_start(w_sb[:, 0], w_t[:, 0]).then_inc(weights_in, 16)
            pool.dma_start(w_sb[:, 1:6], w_t[:, 1:6]).then_inc(weights_in, 16)
            pool.wait_ge(exponent_made, 1)

            def inverse_root(n, width=1):
                pool.wait_ge(stats_ready, n)
                nc.gpsimd.tensor_tensor(rstd[:, 0:width], var_eps[:, 0:width], neg_half[:, 0:width],
                                        ALU.pow).then_inc(rstd_ready, 1)

            def spread_queries(b, parity):
                for src, dst in ((q_hi, qbd_hi), (q_lo, qbd_lo)):
                    nc.gpsimd.tensor_tensor(
                        dst[:, parity],
                        src[:, :, bass.ds(b * Q, Q)].bitcast(F32).unsqueeze(2).broadcast_to([P, G, HG, Q]),
                        mask_sb[:, 0:HG].unsqueeze(1).unsqueeze(3).broadcast_to([P, G, HG, Q]),
                        ALU.mult).then_inc(qbd_ready, 1)

            inverse_root(1, TT)
            pool.wait_ge(consts_made, CONSTS_MADE)
            pool.wait_ge(weights_in, 48)
            pool.wait_ge(q_split, 1)
            spread_queries(0, 0)

            def tile(t, units, chain):
                for s in range(STEPS):
                    bi, k = divmod(s, KT)
                    b = 2 * t + bi
                    n = b * KT + k
                    pool.wait_ge(exp_done, n + 1)
                    if k == 0:
                        if not is_first(b):
                            pool.wait_ge(denom_done, b)
                        acc = zero[:, 0:1].broadcast_to([P, G * 512])
                    else:
                        pool.wait_ge(summed, n)
                        acc = prob_sum[0:ROWS[k], :]
                    nc.gpsimd.tensor_tensor(prob_sum[0:ROWS[k], :], probs[0:ROWS[k], s % 2, :], acc[0:ROWS[k]],
                                            ALU.add).then_inc(summed, 1)
                    if k == 2 and any(kind == "M" for j in range(KT) for _, kind, _ in units.at[bi * KT + j]):
                        spread_queries(b + 1, (bi + 1) % 2)
                    if chain and "y1" in CHAIN_AT.get(s, []):
                        inverse_root(2 * t)
                    if chain and "y2" in CHAIN_AT.get(s, []):
                        inverse_root(2 * t + 1)

            tile(0, FIRST, False)
            with pool.Fori(1, TT - 1) as t:
                tile(t, MIDDLE(t), True)
            tile(TT - 1, LAST, True)
            inverse_root(2 * TT)
            inverse_root(2 * TT + 1)

        @block.scalar
        def _(act):
            def split_hi(b, c):
                act.wait_ge(ctx_in[c % 2], 16 * (2 * b + c // 2 + 1))
                nc.scalar.activation(ctx_hi[:, :, EDGE[c]:EDGE[c + 1]], ctx_raw[:, c % 2, :, 0:EDGE[c + 1] - EDGE[c]],
                                     ACT.Copy).then_inc(ctx_hi_done, 1)

            def unit(units, n, kind, u, t, b, parity):
                if kind == "M" or kind in ("y1", "s0", "s1", "o0", "o1", "y2", "b2"):
                    return
                src = bank[:, UNIT + n % RING, :]
                units.wait_filled(act, filled, n)
                if kind == "K":
                    c, g = divmod(u, G)
                    nc.scalar.activation(k_hi[:, parity, g, EDGE[c]:EDGE[c + 1]], src[:, EDGE[c] - CH[c]:CW],
                                         ACT.Identity, bias=bias_sb[:, 1, g:g + 1]).then_inc(k_hi_done, 1)
                elif kind == "V":
                    nc.scalar.activation(v_sb[0:ROWS[u], parity, u * D:u * D + D], src[0:ROWS[u], 0:D],
                                         ACT.Copy).then_inc(read_act, 1)
                elif kind == "xt1":
                    nc.scalar.activation(xn_t[:, :, :].rearrange("p c n -> p (c n)"), src[:, 0:D],
                                         ACT.Copy).then_inc(read_act, 1)
                elif kind == "qk":
                    nc.scalar.activation(k2_t[:, :, :], src[:, G * P:2 * G * P].rearrange("p (g n) -> p g n", g=G),
                                         ACT.Copy)
                    nc.scalar.activation(q2_t[:, :, :], src[:, 0:G * P].rearrange("p (g n) -> p g n", g=G),
                                         ACT.Copy, scale=SCALE).then_inc(read_act, 1)
                elif kind == "v":
                    nc.scalar.activation(v2[:, :], src[:, 0:D], ACT.Copy).then_inc(read_act, 1)
                elif kind.startswith("st"):
                    bi, g = int(kind[2]), int(kind[3])
                    rows = slice(bi * Q, bi * Q + Q)
                    nc.scalar.activation(probs2[rows, g * 512:g * 512 + 512], src[rows, :], ACT.Exp)\
                        .then_inc(read_act, 1)
                elif kind == "xt2":
                    nc.scalar.activation(xn_t[:, :, :].rearrange("p c n -> p (c n)"), src[:, 0:D],
                                         ACT.Copy).then_inc(read_act, 1)
                    act.wait_ge(read_act, units.before[1] + units.counts(n + 1)[1])
                    nc.scalar.activation(xn2_hi[:, :, bass.ds(t * P, P)], xn_t[:, :, :], ACT.Copy)\
                        .then_inc(xn2_hi_done, 1)
                elif kind == "router":
                    act.wait_ge(negmax_ready, t + 1)
                    nc.scalar.activation(logits[:, :], src[:, 0:E], ACT.Exp, bias=row_max[:, :],
                                         accum_out=row_sum[:, :]).then_inc(read_act, 1)
                elif kind == "gt":
                    nc.scalar.activation(gates_t[:, :], src[0:E, 0:P], ACT.Copy).then_inc(read_act, 1)

            act.wait_ge(consts_in, CONST_DMAS * 16)
            act.wait_ge(consts_made, CONSTS_MADE)
            split_hi(0, 0)
            split_hi(0, 1)
            act.wait_ge(xt_psum, 1)
            nc.scalar.activation(xn_all_t, bank[:, 0:DC, :], ACT.Copy).then_inc(xt_ready, 1)
            act.wait_ge(q_psum, 1)
            for g in range(G):
                nc.scalar.activation(q_all[:, g, :], bank[:, 2 + g, :], ACT.Identity, bias=bq_scaled[:, g:g + 1],
                                     scale=SCALE).then_inc(q_ready, 1)
            act.wait_ge(q_ready, G)
            nc.scalar.activation(q_hi[:, :, :], q_all, ACT.Copy).then_inc(q_hi_done, 1)

            for k in range(KT):
                for c in SPLIT_AT.get(k, []):
                    if c > 1:
                        split_hi(0, c)
                for n, kind, u in PROLOGUE.at[k]:
                    unit(PROLOGUE, n, kind, u, 0, 0, 0)

            def tile(t, units, more):
                for s in range(STEPS):
                    bi, k = divmod(s, KT)
                    b = 2 * t + bi
                    n = b * KT + k
                    act.wait_ge(scores_done, n + 1)
                    if not (is_first(b) and k < 2):
                        act.wait_ge(pv_done, n - 1)
                        act.wait_ge(summed, n - 1)
                    nc.scalar.activation(probs[0:ROWS[k], s % 2, :].rearrange("p (g n) -> p g n", g=G),
                                         bank[0:ROWS[k], 2 * (s % 2):2 * (s % 2) + 2, :], ACT.Exp).then_inc(exp_done, 1)
                    if more > bi:
                        for c in SPLIT_AT.get(k, []):
                            split_hi(b + 1, c)
                    for m, kind, u in units.at[s]:
                        unit(units, m, kind, u, t - 1, b + 1, (bi + 1) % 2)

            tile(0, FIRST, 2)
            with act.Fori(1, TT - 1) as t:
                tile(t, MIDDLE(t), 2)
            tile(TT - 1, LAST, 1)

            def split_w(i, count, j):
                w, part = divmod(j, PIECES)
                if j == 0:
                    act.wait_ge(w_in[i], count)
                at = slice(part * PIECE, part * PIECE + PIECE)
                nc.scalar.activation(w_hi[i][:, w, at], raw_sb[i][:, w, at], ACT.Copy).then_inc(w_hi_done, 1)

            for s in range(STEPS):
                if s in SPLIT_W_AT:
                    act.wait_ge(denom_done, B)
                    split_w(0, 32, SPLIT_W_AT.index(s))
                for m, kind, u in TAIL.at[s]:
                    unit(TAIL, m, kind, u, TT - 1, B, 0)

            def experts(p, more):
                for i in range(2):
                    e = 2 * p + i
                    for c in range(HC):
                        n = e * HC + c
                        act.wait_ge(h_psum, n + 1)
                        if not (is_first(p) and i == 0 and c < 2):
                            act.wait_ge(h_split, n - 1)
                        nc.scalar.activation(h_raw[:, c % 2, :], bank[:, c % 4, :], ACT.Gelu,
                                             bias=b1_sb[:, bass.ds(e, 1), c:c + 1].rearrange("p a b -> p (a b)"))\
                            .then_inc(h_ready, 1)
                        if i == 0 or more:
                            if c == PIECES and not (is_first(p) and i == 0):
                                act.wait_ge(y_chunk, e * HC)
                            split_w((i + 1) % 2, 32 * (p + 1 + i), c)

            experts(0, True)
            with act.Fori(1, E // 2 - 1) as p:
                experts(p, True)
            experts(E // 2 - 1, False)

        @block.vector
        def _(dve):
            links = [0, 0]

            def link(ins):
                links[0] += 1
                ins.then_inc(dve_step, 1)
                dve.wait_ge(dve_step, links[1] + links[0])

            def statistics(src, at=0):
                link(nc.vector.bn_stats(stats[:, at, :], src))
                nc.vector.memset(unused[:, :], 0.0)
                link(nc.vector.bn_aggr(mean_var[:, at, :], stats[:, at, :]))

            def normalize(dst, src, n, done, at=0):
                dve.wait_ge(rstd_ready, n)
                nc.vector.tensor_scalar(dst, src, mean_var[:, at, 0:1], rstd[:, at:at + 1], ALU.subtract,
                                        ALU.mult).then_inc(done, 1)

            def split_lo(b, c):
                dve.wait_ge(ctx_hi_done, b * NC + c + 1)
                nc.vector.tensor_tensor(ctx_lo[:, :, EDGE[c]:EDGE[c + 1]], ctx_raw[:, c % 2, :, 0:EDGE[c + 1] - EDGE[c]],
                                        ctx_hi[:, :, EDGE[c]:EDGE[c + 1]].bitcast(F32),
                                        ALU.subtract).then_inc(ctx_lo_done, 1)

            def finish_heads(src, dst, done, freed=None):
                both = src.rearrange("p (w s q) -> p w s q", w=2 * G, s=2)
                link(nc.vector.tensor_scalar(odd[:, :, :], both[:, :, 1, :], mask_sb[:, HG + 1:HG + 2], None, ALU.mult))
                ins = nc.vector.scalar_tensor_tensor(out=own[:, :, :], in0=both[:, :, 0, :], scalar=mask_sb[:, HG:HG + 1],
                                                     in1=odd[:, :, :], op0=ALU.mult, op1=ALU.add)
                if freed is None:
                    link(ins)
                else:
                    ins.then_inc(read_dve, 1)
                    dve.wait_ge(read_dve, freed)
                link(nc.vector.reciprocal(own[:, G:2 * G, :], own[:, G:2 * G, :]))
                nc.vector.tensor_tensor(dst, own[:, 0:G, :], own[:, G:2 * G, :], ALU.mult).then_inc(done, 1)

            def on_diagonal(dst, values, done):
                nc.vector.tensor_tensor(dst, ident[:, :].unsqueeze(1).broadcast_to([P, G * PAIRS, P]),
                                        values.unsqueeze(2).broadcast_to([P, G * PAIRS, P]), ALU.mult).then_inc(done, 1)

            def spread_own_queries(bi):
                nc.vector.tensor_tensor(
                    qbd2[:, :, :, :], q2_t[:, :, bi * Q:bi * Q + Q].unsqueeze(2).broadcast_to([P, G, HG, Q]),
                    mask_sb[:, 0:HG].unsqueeze(1).unsqueeze(3).broadcast_to([P, G, HG, Q]),
                    ALU.mult).then_inc(qbd2_ready, 1)

            def unit(units, n, kind, u, t, b, parity):
                src = bank[:, UNIT + n % RING, :]
                if kind == "K":
                    c, g = divmod(u, G)
                    dve.wait_ge(k_hi_done, b * K_UNITS + u + 1)
                    nc.vector.scalar_tensor_tensor(
                        out=k_lo[:, parity, g, EDGE[c]:EDGE[c + 1]], in0=src[:, EDGE[c] - CH[c]:CW],
                        scalar=bias_sb[:, 1, g:g + 1], in1=k_hi[:, parity, g, EDGE[c]:EDGE[c + 1]].bitcast(F32),
                        op0=ALU.add, op1=ALU.subtract).then_inc(read_dve, 1)
                elif kind == "router":
                    units.wait_filled(dve, filled, n)
                    nc.vector.tensor_reduce(row_max[:, :], src[:, 0:E], AX.X, ALU.max, negate=True)\
                        .then_inc(negmax_ready, 1)
                elif kind == "xt2":
                    dve.wait_ge(xn2_hi_done, t + 1)
                    nc.vector.tensor_tensor(xn2_lo[:, :, bass.ds(t * P, P)], xn_t[:, :, :],
                                            xn2_hi[:, :, bass.ds(t * P, P)].bitcast(F32), ALU.subtract)
                if kind in READ_BY_ACT or kind == "K":
                    return
                units.wait_filled(dve, filled, n)
                if kind == "M":
                    pair, c = divmod(u, NC)
                    nc.vector.tensor_reduce(maxes[:, pair, c:c + 1], src[:, 0:CW], AX.X, ALU.max).then_inc(read_dve, 1)
                elif kind in ("y1", "y2"):
                    x_tile = x_all[:, bass.ds(t, 1), :].rearrange("p a n -> p (a n)")
                    nc.vector.tensor_tensor(x1[:, :], src[:, 0:D], x_tile if kind == "y1" else x1[:, :],
                                            ALU.add).then_inc(read_dve, 1)
                    dve.wait_ge(read_dve, units.before[2] + units.counts(n + 1)[2])
                    statistics(x1[:, :])
                    nc.vector.tensor_scalar(var_eps[:, 0:1], mean_var[:, 0, 1:2], EPS, None,
                                            ALU.add).then_inc(stats_ready, 1)
                elif kind in ("s0", "s1"):
                    nc.vector.tensor_tensor(masked[:, :, :], src.rearrange("p (n k) -> p n k", k=Q),
                                            causal_sb[:, :].unsqueeze(1).broadcast_to([P, G * PAIRS, Q]),
                                            ALU.add).then_inc(read_dve, 1)
                    dve.wait_ge(read_dve, units.before[2] + units.counts(n + 1)[2])
                    link(nc.vector.tensor_reduce(neg_max2[:, :], masked[:, :, :], AX.X, ALU.max, negate=True))
                    on_diagonal(shift2[:, :, :], neg_max2[:, :], shift2_ready)
                elif kind in ("o0", "o1"):
                    bi = int(kind[1])
                    finish_heads(src, o2_t[:, :, bi * Q:bi * Q + Q], o2_ready, units.before[2] + units.counts(n + 1)[2])
                elif kind == "b2":
                    x_tile = x_all[:, bass.ds(t, 1), :].rearrange("p a n -> p (a n)")
                    nc.vector.tensor_tensor(x_tile, x1[:, :], src[:, 0:D], ALU.add).then_inc(read_dve, 1)
                    nc.vector.memset(unused[:, :], 0.0).then_inc(tile_done, 1)

            def route(units, t):
                units.wait_read_act(dve, read_act, "router")
                link(nc.vector.reciprocal(row_sum[:, :], row_sum[:, :]))
                link(nc.vector.tensor_scalar(logits[:, :], logits[:, :], row_sum[:, :], None, ALU.mult))
                mine = logits[:, :].unsqueeze(2).broadcast_to([P, E, E])
                other = logits[:, :].unsqueeze(1).broadcast_to([P, E, E])
                link(nc.vector.tensor_tensor(above[:, :, :], other, mine, ALU.is_gt))
                link(nc.vector.tensor_tensor(ties[:, :, :], other, mine, ALU.is_equal))
                link(nc.vector.tensor_tensor(ties[:, :, :], ties[:, :, :], earlier[:, :, :], ALU.mult))
                link(nc.vector.tensor_tensor(above[:, :, :], above[:, :, :], ties[:, :, :], ALU.add))
                link(nc.vector.tensor_reduce(rank[:, :], above[:, :, :], AX.X, ALU.add))
                nc.vector.scalar_tensor_tensor(out=gate_tile[:, :], in0=rank[:, :], scalar=1.5, in1=logits[:, :],
                                               op0=ALU.is_lt, op1=ALU.mult).then_inc(gates_ready, 1)
                dve.wait_ge(gates_ready, t + 1)
                nc.vector.tensor_copy(gates[:, bass.ds(t, 1), :].rearrange("p a n -> p (a n)"), gate_tile[:, :])

            def chain_between(units, s, t):
                if "y1" in CHAIN_AT.get(s - 1, []):
                    normalize(xn[:, :], x1[:, :], 2 * t + 2, xn1_ready)
                if "y2" in CHAIN_AT.get(s - 1, []):
                    normalize(xn[:, :], x1[:, :], 2 * t + 3, xn2_ready)
                for bi, after in ((0, "qk"), (1, "st01")):
                    if after in CHAIN_AT.get(s - 1, []):
                        units.wait_read_act(dve, read_act, after)
                        spread_own_queries(bi)
                if "router" in CHAIN_AT.get(s - 1, []):
                    route(units, t)

            dve.wait_ge(x_in, 16)
            for t in range(TT):
                statistics(x_all[:, t, :], t)
            nc.vector.tensor_scalar(var_eps[:, :], mean_var[:, :, 1], EPS, None, ALU.add).then_inc(stats_ready, 1)
            dve.wait_ge(kv_weights_in, 16)
            for w, hi, lo in ((0, wk_hi, wk_lo), (1, wv_hi, wv_lo)):
                link(nc.vector.tensor_copy(hi[:, :, :], w_raw[:, w]))
                nc.vector.tensor_tensor(lo[:, :, :], w_raw[:, w], hi[:, :, :].bitcast(F32),
                                        ALU.subtract).then_inc(kv_weights_split, 1)
            for t in range(TT):
                normalize(xn_all[:, t, :], x_all[:, t, :], 1, xn_ready, t)
            dve.wait_ge(consts_in, CONST_DMAS * 16)
            nc.vector.tensor_copy(ident_bf[:, :], ident[:, :]).then_inc(consts_made, 1)
            nc.vector.tensor_scalar(bq_scaled[:, :], bias_sb[:, 0, :], SCALE, None, ALU.mult).then_inc(consts_made, 1)
            nc.vector.tensor_copy(causal_bf[:, :], causal_sb[:, :])
            split_lo(0, 0)
            split_lo(0, 1)
            link(nc.vector.memset(earlier[:, :, :], 0.0))
            for e in range(1, E):
                nc.vector.memset(earlier[:, e, 0:e], 1.0)
            dve.wait_ge(bo_psum, 1)
            dve.wait_ge(weights_in, 48)
            link(nc.vector.tensor_tensor(bo_all[:, :], bank[0:1, O, 0:D], bo_sb[:, :], ALU.add))
            dve.wait_ge(q_hi_done, 1)
            nc.vector.tensor_tensor(q_lo[:, :, :], q_all, q_hi[:, :, :].bitcast(F32), ALU.subtract).then_inc(q_split, 1)

            def find_shift(parity):
                link(nc.vector.tensor_reduce(neg_max[:, :], maxes[:, :, :], AX.X, ALU.max, negate=True))
                on_diagonal(shift[:, parity], neg_max[:, :], shift_ready)

            for k in range(KT):
                for c in SPLIT_AT.get(k, []):
                    if c > 1:
                        split_lo(0, c)
                for n, kind, u in PROLOGUE.at[k]:
                    unit(PROLOGUE, n, kind, u, 0, 0, 0)
            dve.wait_ge(read_dve, PROLOGUE.total()[2])
            find_shift(0)

            def tile(t, units, more, chain):
                for s in range(STEPS):
                    bi, k = divmod(s, KT)
                    b = 2 * t + bi
                    if k == 1 and not is_first(b):
                        dve.wait_ge(denom_done, b)
                        at = (bi + 1) % 2 * Q
                        finish_heads(bank[:, O, :], o_t[:, :, at:at + Q], o_ready)
                    if k == KT - 1 and more > bi:
                        n = max(n for j in range(s) for n, kind, _ in units.at[j] if kind == "M")
                        dve.wait_ge(read_dve, units.before[2] + units.counts(n + 1)[2])
                        find_shift((bi + 1) % 2)
                    if more > bi:
                        for c in SPLIT_AT.get(k, []):
                            split_lo(b + 1, c)
                    if chain:
                        chain_between(units, s, t - 1)
                    for m, kind, u in units.at[s]:
                        unit(units, m, kind, u, t - 1, b + 1, (bi + 1) % 2)

            tile(0, FIRST, 2, False)
            start = links[0]
            with dve.Fori(1, TT - 1) as t:
                links[0] = start
                links[1] = (t - 1) * TILE_LINKS
                tile(t, MIDDLE(t), 2, True)
            assert links[0] == start + TILE_LINKS, links[0] - start
            links[:] = [start + (TT - 2) * TILE_LINKS, 0]
            tile(TT - 1, LAST, 1, True)
            dve.wait_ge(denom_done, B)
            finish_heads(bank[:, O, :], o_t[:, :, Q:2 * Q], o_ready)

            def split_w(i, n, j):
                w, part = divmod(j, PIECES)
                at = slice(part * PIECE, part * PIECE + PIECE)
                dve.wait_ge(w_hi_done, n + 1)
                nc.vector.tensor_tensor(w_lo[i][:, w, at], raw_sb[i][:, w, at], w_hi[i][:, w, at].bitcast(F32),
                                        ALU.subtract).then_inc(w_split, 1)

            def gated_sum(e, i):
                for t in range(TT):
                    ins = nc.vector.scalar_tensor_tensor(
                        out=x_all[:, t, :], in0=bank[:, 4 + 2 * i + t // 2, (t % 2) * D:(t % 2) * D + D],
                        scalar=gates[:, t, bass.ds(e, 1)], in1=x_all[:, t, :], op0=ALU.mult, op1=ALU.add)
                ins.then_inc(y_taken, 1)

            for s in range(STEPS):
                if s in SPLIT_W_AT:
                    split_w(0, SPLIT_W_AT.index(s), SPLIT_W_AT.index(s))
                chain_between(TAIL, s, TT - 1)
                for m, kind, u in TAIL.at[s]:
                    unit(TAIL, m, kind, u, TT - 1, B, 0)

            def experts(p, more):
                for i in range(2):
                    e = 2 * p + i
                    for c in range(HC):
                        n = e * HC + c
                        dve.wait_ge(h_ready, n + 1)
                        if not (is_first(p) and i == 0 and c < 4):
                            dve.wait_ge(y_chunk, n - 3)
                        link(nc.vector.tensor_copy(h_hi[:, c % 4, :], h_raw[:, c % 2, :]))
                        nc.vector.tensor_tensor(h_lo[:, c % 4, :], h_raw[:, c % 2, :], h_hi[:, c % 4, :].bitcast(F32),
                                                ALU.subtract).then_inc(h_split, 1)
                        if i == 0 or more:
                            split_w((i + 1) % 2, (e + 1) * 2 * PIECES + c, c)
                        if c == 2 and not (is_first(p) and i == 0):
                            dve.wait_ge(y_chunk, e * HC)
                            gated_sum(e - 1, (i + 1) % 2)

            experts(0, True)
            start = links[0]
            per = 2 * HC
            with dve.Fori(1, E // 2 - 1) as p:
                links[0] = start
                links[1] = (p - 1) * per
                experts(p, True)
            links[:] = [start + (E // 2 - 2) * per, 0]
            experts(E // 2 - 1, False)
            dve.wait_ge(y_chunk, E * HC)
            gated_sum(E - 1, 1)

        @block.tensor
        def _(pe):
            def split_product(dst, pairs, start=True, stop=True, **more):
                n = 0
                for (a_hi, a_lo), (b_hi, b_lo) in pairs:
                    for lhs, rhs in ((a_hi, b_hi), (a_hi, b_lo), (a_lo, b_hi)):
                        n += 1
                        last = nc.tensor.matmul(dst, lhs, rhs, start=(start and n == 1),
                                                stop=(stop and n == 3 * len(pairs)), **more)
                return last

            def weigh_heads(dst_bank, at, lhs, p_rows, start, stop):
                for g in range(G):
                    for j in range(PAIRS):
                        ins = nc.tensor.matmul(dst_bank[32 * j:32 * j + 32, (at + g) * P:(at + g + 1) * P], lhs(g, j),
                                               p_rows[:, (g * PAIRS + j) * P:(g * PAIRS + j + 1) * P],
                                               start=(start and g == 0), stop=stop, skip_group_check=True)
                return ins

            def transposes(dst):
                for c in range(DC):
                    ins = nc.tensor.transpose(dst[:, c * P:c * P + P], xn[:, c * P:c * P + P], ident[:, :])
                return ins

            def unit(units, n, kind, u, t, b, parity):
                dst = bank[:, UNIT + n % RING, :]
                units.wait_free(pe, read_act, read_dve, n)
                if kind == "K":
                    c, g = divmod(u, G)
                    pe.wait_ge(ctx_lo_done, b * NC + c + 1)
                    cols, keys = slice(g * P, g * P + P), slice(CH[c], CH[c] + CW)
                    ins = split_product(dst[:, 0:CW], [((wk_hi[:, d, cols], wk_lo[:, d, cols]),
                                                        (ctx_hi[:, d, keys], ctx_lo[:, d, keys])) for d in range(DC)])
                elif kind == "V":
                    keys = slice(u * P, u * P + ROWS[u])
                    c = next(c for c in range(NC) if EDGE[c + 1] >= keys.stop)
                    pe.wait_ge(ctx_lo_done, b * NC + c + 1)
                    ins = split_product(dst[0:ROWS[u], 0:D], [((ctx_hi[:, d, keys], ctx_lo[:, d, keys]),
                                                               (wv_hi[:, d, :], wv_lo[:, d, :])) for d in range(DC)])
                elif kind == "M":
                    pair, c = divmod(u, NC)
                    g, j = divmod(pair, PAIRS)
                    if u == 0:
                        pe.wait_ge(k_hi_done, (b + 1) * K_UNITS)
                        pe.wait_ge(qbd_ready, 2 * (b + 1))
                    ins = nc.tensor.matmul(dst[:, 0:CW],
                                           qbd_hi[:, parity, g, 2 * j:2 * j + 2, :].rearrange("p s q -> p (s q)"),
                                           k_hi[:, parity, g, CH[c]:CH[c] + CW], start=True, stop=True)
                elif kind == "y1":
                    pe.wait_ge(o_ready, 2 * t + 2)
                    for g in range(G):
                        nc.tensor.matmul(dst[:, 0:D], o_t[:, g, :], w_sb[:, 1, g, :], start=(g == 0), stop=False)
                    ins = nc.tensor.matmul(dst[:, 0:D], ones_f[0:1, :], bo_all[:, :], start=False, stop=True)
                elif kind == "xt1":
                    pe.wait_ge(xn1_ready, t + 1)
                    ins = transposes(dst)
                elif kind == "qk":
                    units.wait_read_act(pe, read_act, "xt1")
                    for w in range(2):
                        for g in range(G):
                            for c in range(DC):
                                ins = nc.tensor.matmul(dst[:, (w * G + g) * P:(w * G + g + 1) * P],
                                                       w_sb[:, 2 + w, c, g * P:g * P + P], xn_t[:, c, :],
                                                       start=(c == 0), stop=(c == DC - 1))
                elif kind == "v":
                    for c in range(DC):
                        ins = nc.tensor.matmul(dst[:, 0:D], xn_t[:, c, :], w_sb[:, 4, c, :], start=(c == 0),
                                               stop=(c == DC - 1))
                elif kind in ("s0", "s1"):
                    bi = int(kind[1])
                    pe.wait_ge(qbd2_ready, 2 * t + bi + 1)
                    units.wait_read_act(pe, read_act, "qk")
                    for g in range(G):
                        for j in range(PAIRS):
                            m = g * PAIRS + j
                            ins = nc.tensor.matmul(dst[:, m * Q:m * Q + Q],
                                                   qbd2[:, g, 2 * j:2 * j + 2, :].rearrange("p s q -> p (s q)"),
                                                   k2_t[:, g, bi * Q:bi * Q + Q], start=True, stop=True)
                elif kind.startswith("st"):
                    bi, g = int(kind[2]), int(kind[3])
                    pe.wait_ge(shift2_ready, 2 * t + bi + 1)
                    half = dst[bi * Q:bi * Q + Q, :]
                    nc.tensor.matmul(half, k2_t[:, g, bi * Q:bi * Q + Q], qbd2[:, g].rearrange("p h q -> p (h q)"),
                                     start=True, stop=False)
                    nc.tensor.matmul(half, ones_bf[:, 0:Q],
                                     shift2[:, g * PAIRS:(g + 1) * PAIRS].rearrange("p j c -> p (j c)"),
                                     start=False, stop=False)
                    ins = nc.tensor.matmul(half, causal_bf[:, :], ident_bf[:, :].unsqueeze(1).broadcast_to([P, PAIRS, P]),
                                           start=False, stop=True)
                elif kind in ("o0", "o1"):
                    bi = int(kind[1])
                    rows = slice(bi * Q, bi * Q + Q)
                    units.wait_read_act(pe, read_act, f"st{bi}1")
                    nc.tensor.matmul(dst[:, 0:E], ones_bf[:, :], ident_bf[:, 0:E], start=True, stop=True)
                    weigh_heads(dst, 0, lambda g, j: v2[rows, g * P + 32 * j:g * P + 32 * j + 32], probs2[rows, :],
                                True, True)
                    ins = weigh_heads(dst, G, lambda g, j: ones_f[rows, 0:32], probs2[rows, :], False, True)
                elif kind == "y2":
                    pe.wait_ge(o2_ready, 2 * (t + 1))
                    for g in range(G):
                        ins = nc.tensor.matmul(dst[:, 0:D], o2_t[:, g, :], w_sb[:, 5, g, :], start=(g == 0),
                                               stop=(g == G - 1))
                elif kind == "xt2":
                    pe.wait_ge(xn2_ready, t + 1)
                    ins = transposes(dst)
                elif kind == "router":
                    units.wait_read_act(pe, read_act, "xt2")
                    for c in range(DC):
                        nc.tensor.matmul(dst[:, 0:E], xn_t[:, c, :], wg_sb[:, c, :], start=(c == 0), stop=False)
                    ins = nc.tensor.matmul(dst[:, 0:E], ones_f[0:1, :], bg_sb[:, :], start=False, stop=True)
                elif kind == "gt":
                    pe.wait_ge(gates_ready, t + 1)
                    ins = nc.tensor.transpose(dst[0:E, 0:P], gate_tile[:, :], ident[:, :])
                elif kind == "b2":
                    units.wait_read_act(pe, read_act, "gt")
                    ins = nc.tensor.matmul(dst[:, 0:D], gates_t[:, :], b2_sb[:, :], start=True, stop=True)
                ins.then_inc(filled, 1)

            def scores(b, bi, k):
                n = b * KT + k
                rows, buf = ROWS[k], (KT * bi + k) % 2
                if not (is_first(b) and k < 2):
                    pe.wait_ge(exp_done, n - 1)
                if k == 0:
                    pe.wait_ge(shift_ready, b + 1)
                keys = slice(k * P, k * P + rows)
                for g in range(G):
                    dst = bank[0:rows, 2 * buf + g, :]
                    hi = qbd_hi[:, bi, g].rearrange("p h q -> p (h q)")
                    lo = qbd_lo[:, bi, g].rearrange("p h q -> p (h q)")
                    split_product(dst, [((k_hi[:, bi, g, keys], k_lo[:, bi, g, keys]), (hi, lo))], stop=False)
                    ins = nc.tensor.matmul(dst, ones_bf[:, 0:rows],
                                           shift[:, bi, g * PAIRS:(g + 1) * PAIRS].rearrange("p j c -> p (j c)"),
                                           start=False, stop=True)
                ins.then_inc(scores_done, 1)

            def weigh(b, bi, k):
                n = b * KT + k
                buf = (KT * bi + k) % 2
                pe.wait_ge(exp_done, n + 1)
                if k == 0 and not is_first(b):
                    pe.wait_ge(o_ready, b)
                rows = slice(0, ROWS[k])
                weigh_heads(bank[:, O, :], 0, lambda g, j: v_sb[rows, bi, k * D + g * P + 32 * j:k * D + g * P + 32 * j + 32],
                            probs[rows, buf, :], k == 0, k == KT - 1).then_inc(pv_done, 1)

            def denominators(b):
                pe.wait_ge(summed, (b + 1) * KT)
                weigh_heads(bank[:, O, :], G, lambda g, j: ones_f[:, 0:32], prob_sum[:, :], False, True)\
                    .then_inc(denom_done, 1)

            pe.wait_ge(consts_in, CONST_DMAS * 16)
            pe.wait_ge(consts_made, CONSTS_MADE)
            pe.wait_ge(weights_in, 48)
            pe.wait_ge(xn_ready, TT)
            for t in range(TT):
                for c in range(DC):
                    ins = nc.tensor.transpose(bank[:, c, t * P:t * P + P], xn_all[:, t, c * P:c * P + P], ident[:, :])
            ins.then_inc(xt_psum, 1)
            for c in range(DC):
                ins = nc.tensor.matmul(bank[0:1, O, 0:D], bias_sb[:, 2, c:c + 1], w_sb[:, 1, c, :], start=(c == 0),
                                       stop=(c == DC - 1))
            ins.then_inc(bo_psum, 1)
            pe.wait_ge(xt_ready, 1)
            for g in range(G):
                for c in range(DC):
                    ins = nc.tensor.matmul(bank[:, 2 + g, :], w_sb[:, 0, c, g * P:g * P + P], xn_all_t[:, c, :],
                                           start=(c == 0), stop=(c == DC - 1))
            ins.then_inc(q_psum, 1)
            pe.wait_ge(kv_weights_split, 2)
            for k in range(KT):
                for n, kind, u in PROLOGUE.at[k]:
                    unit(PROLOGUE, n, kind, u, 0, 0, 0)

            def tile(t, units):
                for s in range(STEPS):
                    bi, k = divmod(s, KT)
                    b = 2 * t + bi
                    if k == 2:
                        weigh(b, bi, 0)
                    scores(b, bi, k)
                    if k == 1 and not is_first(b):
                        denominators(b - 1)
                    for n, kind, u in units.at[s]:
                        unit(units, n, kind, u, t - 1, b + 1, (bi + 1) % 2)
                    if k == 0 and not is_first(b):
                        weigh(b - 1, (bi + 1) % 2, KT - 1)
                    if k >= 2:
                        weigh(b, bi, k - 1)

            tile(0, FIRST)
            with pe.Fori(1, TT - 1) as t:
                tile(t, MIDDLE(t))
            tile(TT - 1, LAST)
            weigh(B - 1, 1, KT - 1)
            denominators(B - 1)
            for s in range(STEPS):
                for n, kind, u in TAIL.at[s]:
                    unit(TAIL, n, kind, u, TT - 1, B, 0)

            def hidden(e, i, c):
                n = e * HC + c
                if not (isinstance(e, int) and e == 0 and c < 4):
                    pe.wait_ge(h_ready, n - 3)
                w = [w_hi[i][:, 0, :].rearrange("p (d n) -> p d n", d=DC), w_lo[i][:, 0, :].rearrange("p (d n) -> p d n", d=DC)]
                cols = slice(c * P, c * P + P)
                split_product(bank[:, c % 4, :], [((w[0][:, d, cols], w[1][:, d, cols]), (xn2_hi[:, d, :], xn2_lo[:, d, :]))
                                                  for d in range(DC)]).then_inc(h_psum, 1)

            def output(n, i, c):
                pe.wait_ge(h_split, n + 1)
                cols = slice(c * D, c * D + D)
                for t in range(TT):
                    toks = slice(t * P, t * P + P)
                    ins = split_product(bank[:, 4 + 2 * i + t // 2, (t % 2) * D:(t % 2) * D + D],
                                        [((h_hi[:, c % 4, toks], h_lo[:, c % 4, toks]), (w_hi[i][:, 1, cols], w_lo[i][:, 1, cols]))],
                                        start=(c == 0 and t % 2 == 0), stop=(c == HC - 1), skip_group_check=True)
                ins.then_inc(y_chunk, 1)

            pe.wait_ge(tile_done, TT)

            def experts(p):
                for i in range(2):
                    e = 2 * p + i
                    for c in range(HC):
                        if c == 0:
                            pe.wait_ge(w_split, e * 2 * PIECES + PIECES)
                        hidden(e, i, c)
                        if c >= 2:
                            if c == 2:
                                pe.wait_ge(w_split, e * 2 * PIECES + 2 * PIECES)
                            if c == 2 and not (is_first(p)):
                                pe.wait_ge(y_taken, e - 1)
                            output(e * HC + c - 2, i, c - 2)
                        elif not (is_first(p) and i == 0):
                            output(e * HC + c - 2, (i + 1) % 2, HC + c - 2)

            experts(0)
            with pe.Fori(1, E // 2) as p:
                experts(p)
            for c in (HC - 2, HC - 1):
                output((E - 1) * HC + c, 1, c)


def kernel(**a):
    import numpy as np
    import concourse.bacc as bacc
    from concourse.bass_utils import run_bass_kernel_spmd

    def t(w):
        w = np.asarray(w)
        return w.T.reshape(DC, P, -1).transpose(1, 0, 2)

    f = {k: np.asarray(v) for k, v in a.items()}
    wi = f["L0_attn_in_proj_weight"]
    ctx = f["ctx_1024"].transpose(0, 2, 1).reshape(B, DC, P, S).transpose(0, 2, 1, 3)
    weights = np.stack([t(f["L0_xattn_Wq"]), t(f["L0_xattn_Wo"]), t(wi[0:D]), t(wi[D:2 * D]), t(wi[2 * D:3 * D]),
                        t(f["L0_attn_out_proj_weight"]), t(f["L0_xattn_Wk"]), t(f["L0_xattn_Wv"])], 1)
    biases = np.stack([f["L0_xattn_" + n].reshape(DC, P).T for n in ("bq", "bk", "bv")], 1)
    row = np.arange(P)
    head = (row[:, None] // DK == np.arange(HG)[None]).astype(np.float32)
    parity = (row[:, None] // DK % 2 == np.arange(2)[None]).astype(np.float32)
    hidden = np.where(np.arange(Q)[None] > (row % Q)[:, None], np.float32(FAR), np.float32(0))
    arrays = {
        "x": f["x"].reshape(TT, P, D).transpose(1, 0, 2),
        "ctx_t": ctx, "w_t": weights, "wg_t": t(f["L0_ffn_Wg"].T), "biases": biases,
        "bo_row": f["L0_xattn_bo"][None], "bg_row": f["L0_ffn_bg"][None],
        "w1": f["L0_ffn_W1"].reshape(E, DC, P, HID).transpose(0, 2, 1, 3),
        "b1": f["L0_ffn_b1"].reshape(E, HC, P).transpose(2, 0, 1),
        "w2": f["L0_ffn_W2"].reshape(E, HC, P, D).transpose(0, 2, 1, 3),
        "b2": f["L0_ffn_b2"],
        "eye": np.eye(P, dtype=np.float32), "masks": np.concatenate([head, parity], 1), "causal": hidden,
    }
    nc = bacc.Bacc("TRN2", target_bir_lowering=False, num_devices=1)
    args, feeds = [], {}
    for name, v in arrays.items():
        v = np.ascontiguousarray(v)
        feeds["in_" + name] = v
        args.append(nc.dram_tensor("in_" + name, v.shape, mybir.dt.from_np(v.dtype), kind="ExternalInput").ap())
    out = nc.dram_tensor("result", (P, TT, D), F32, kind="ExternalOutput").ap()
    perceiver_kernel(nc, *args, out)
    r = run_bass_kernel_spmd(nc, [feeds], core_ids=[0])
    return r.results[0]["result"].transpose(1, 0, 2).reshape(B, Q, D)
```

```python
from contextlib import ExitStack

import concourse.bass as bass
from concourse import mybir

F32 = mybir.dt.float32
F32R = mybir.dt.float32r
BF16 = mybir.dt.bfloat16
ACT = mybir.ActivationFunctionType
ALU = mybir.AluOpType
AX = mybir.AxisListType

P = 128
B, Q, D = 8, 64, 256
S = 1601
H, DK = 16, 16
DC = D // P
HG = P // DK
G = H // HG
PAIRS = HG // 2
TOK = B * Q
TT = TOK // P
KT = -(-S // P)
ROWS = [min(P, S - P * k) for k in range(KT)]
CW = 402
CH = [0, 400, 800, S - CW]
NC = len(CH)
EDGE = [0] + [c + CW for c in CH]
HALVES = [(0, EDGE[NC // 2]), (EDGE[NC // 2], S)]
PARTS = 3
K_STACK = [(0, 3), (0, 2), (0, 1)]
Q_STACK = [0, 0, 0, 1, 1, 2]
STACK = len(Q_STACK) * DK
E, HID = 8, 1024
HC = HID // P
EPS = 1e-5
SCALE = 0.25
FAR = -1e30
STEPS = 2 * KT
CONST_DMAS, LATE_DMAS = 2, 6
CONSTS_MADE = 4
RING = 3
TILE_LINKS = 23
K_UNITS = G * NC
PIECES = 4
PIECE = DC * HID // PIECES

K_AT = {0: [0, 1], 1: [2, 3], 2: [4, 5], 4: [6, 7]}
V_AT = {2: [0, 1]} | {k: [k - 1] for k in range(3, KT)}
M_COUNT = {2: 3, 3: 4, 4: 4, 5: 4, 6: 4, 7: 4, 8: 3, 9: 3, 10: 3}
M_AT = {k: range(sum(n for j, n in M_COUNT.items() if j < k), sum(n for j, n in M_COUNT.items() if j <= k))
        for k in M_COUNT}
SPLIT_AT = {2: (1, 3), 6: (2, 0), 8: (2, 1), 10: (2, 2)}
FIRST_K = {0: [0, 1], 1: [2, 3], 2: [4, 5], 3: [6, 7]}
FIRST_V = {2: [0], 3: [1], 4: [2], 5: [3, 4], 6: [5, 6], 7: [7, 8], 8: [9], 9: [10], 10: [11]}
FIRST_M = {2: range(0, 3), 3: range(3, 6), 4: range(6, 10), 5: range(10, 14), 6: range(14, 18), 7: range(18, 22),
           8: range(22, 26), 9: range(26, 29), 10: range(29, 32)}
FIRST_SPLIT = {0: [(0, 0), (0, 1)], 1: [(0, 2)], 2: [(0, 3)], 6: [(1, 0)], 8: [(1, 1)], 9: [(1, 2)]}
FIRST_STEPS = 12
LOAD_AT = [1, 4, 8, 10]
SHIFT_AT = KT - 1
LAST_V_AT = 1
CHAIN_AT = {3: ["y1"], 5: ["xt1"], 6: ["qk", "v"], 8: ["s0"], 10: ["st00", "st01"], 12: ["s1"], 13: ["st10", "st11"],
            15: ["o0"], 16: ["o1"], 19: ["y2"], 21: ["xt2"], 22: ["router"], 24: ["gt"], 25: ["b2"]}
CHAIN_AT_LAST = {2: ["y1"], 4: ["xt1"], 5: ["qk", "v"], 7: ["s0"], 8: ["st00", "st01"], 10: ["s1"],
                 11: ["st10", "st11"], 12: ["o0", "o1"], 14: ["y2"], 16: ["xt2"], 17: ["router"], 19: ["gt"],
                 20: ["b2"]}
CHAIN_ALONE = {0: ["y1"], 2: ["xt1"], 3: ["qk", "v"], 5: ["s0", "s1"], 6: ["st00", "st01"], 7: ["st10", "st11"],
               8: ["o0"], 9: ["o1"], 11: ["y2"], 13: ["xt2"], 14: ["router"], 16: ["gt"], 17: ["b2"]}
SPLIT_W_AT = [5, 6, 7, 8, 9, 10, 11, 12]
FIRST_EXPERT_AT = [1, 2, 4, 7, 8, 10, 11, 12]
HALF = TT // 2
AFTER_WEIGHING = {"V", "VL"}
READ_BY_ACT = {"v", "V", "VL", "X", "xt1", "qk", "st00", "st01", "st10", "st11", "xt2", "router", "gt"}


class Units:

    def __init__(self, before, batch_after, chain, own=True, after_shift=len(V_AT[SHIFT_AT])):
        chain = chain or {}
        self.chain = chain
        self.after_shift = after_shift
        self.before = before
        self.at = {}
        self.ahead = {}
        order = []
        for s in range(STEPS):
            bi, k = divmod(s, KT)
            self.ahead[s], row = step_units(k, own, batch_after > bi, chain.get(s, []))
            self.at[s] = []
            for kind, u in row:
                self.at[s].append((len(order), kind, u))
                order.append(kind)
        self.by_act = [k in READ_BY_ACT for k in order]

    def counts(self, n):
        a = sum(self.by_act[:n])
        return n, a, n - a

    def total(self):
        return self.counts(len(self.by_act))

    def wait_filled(self, eng, sem, n):
        eng.wait_ge(sem, self.before[0] + n + 1)

    def wait_read_act(self, eng, by_act, kind):
        n = next(n for s in range(STEPS) for n, k, _ in self.at[s] if k == kind)
        eng.wait_ge(by_act, self.before[1] + self.counts(n + 1)[1])

    def wait_shift(self, eng, by_act, bi):
        if bi == 0:
            eng.wait_ge(by_act, self.before[1] - self.after_shift)
        else:
            n = max(n for s in range(KT) for n, kind, _ in self.at[s] if kind == "X")
            eng.wait_ge(by_act, self.before[1] + self.counts(n + 1)[1])

    def wait_free(self, eng, by_act, by_dve, n):
        if n < RING:
            if n == 0 and not (isinstance(self.before[1], int) and self.before[1] == 0):
                eng.wait_ge(by_act, self.before[1])
                eng.wait_ge(by_dve, self.before[2])
            return
        a, d = self.counts(n - RING + 1)[1:]
        if self.by_act[n - RING]:
            eng.wait_ge(by_act, self.before[1] + a)
        else:
            eng.wait_ge(by_dve, self.before[2] + d)


def alternate(a, b):
    row = []
    while a or b:
        row += a[:1] + b[:1]
        a, b = a[1:], b[1:]
    return row


def step_units(k, own, following, chain):
    m = [("M", u) for u in M_AT.get(k, [])] if following else []
    if following and k == SHIFT_AT:
        m = [("X", g) for g in range(G)]
    others = [("K", u) for u in K_AT.get(k, [])] if following else []
    others += [(c, 0) for c in chain]
    row = m[:2] + alternate(others, m[2:])
    ahead = len(m[:2])
    row += [("VL", KT - 1)] if own and k == LAST_V_AT else []
    row += [("V", u) for u in V_AT.get(k, [])] if following else []
    return ahead, row


def add(a, b, times=1):
    return tuple(x + times * y for x, y in zip(a, b))


def runs():
    prologue = Units((0, 0, 0), 0, None, False)
    order = []
    for s in range(FIRST_STEPS):
        others = [("K", u) for u in FIRST_K.get(s, [])] + [("V", u) for u in FIRST_V.get(s, [])]
        row = alternate(others, [("M", u) for u in FIRST_M.get(s, [])])
        if s == FIRST_STEPS - 1:
            row = [("X", g) for g in range(G)]
        prologue.at[s] = [(len(order) + i, *r) for i, r in enumerate(row)]
        order += [kind for kind, _ in row]
    prologue.by_act = [k in READ_BY_ACT for k in order]
    first = Units(prologue.total(), 2, None, after_shift=0)
    start = add(first.before, first.total())
    middle_total = Units(start, 2, CHAIN_AT).total()

    def middle(t):
        return Units(add(start, middle_total, t - 1), 2, CHAIN_AT)

    last = Units(add(start, middle_total, TT - 2), 1, CHAIN_AT_LAST)
    tail = Units(add(last.before, last.total()), 0, CHAIN_ALONE, False)
    return prologue, first, middle, last, tail


PROLOGUE, FIRST, MIDDLE, LAST, TAIL = runs()


def perceiver_kernel(nc, x, ctx_t, w_t, wg_t, biases, bo_row, bg_row, w1, b1, w2, b2, eye, masks, causal, out):
    stack = ExitStack()
    with stack:
        def sem(name):
            return stack.enter_context(nc.semaphore(name))

        def sb(name, shape, dt=F32, where=stack):
            return where.enter_context(nc.sbuf_tensor(name, shape, dt))

        ident = sb("ident", [P, P])
        ones_bf = sb("ones_bf", [P, P], BF16)
        ident_bf = sb("ident_bf", [P, P], BF16)
        ones_f = sb("ones_f", [P, P])
        zero = sb("zero", [P, 1])
        neg_half = sb("neg_half", [P, TT])
        unused = sb("unused", [P, 1])
        mask_sb = sb("mask_sb", [P, HG + 2])
        bias_sb = sb("bias_sb", [P, 3, DC])
        bo_sb = sb("bo_sb", [1, D])
        bo_all = sb("bo_all", [1, D])
        bg_sb = sb("bg_sb", [1, E])
        wg_sb = sb("wg_sb", [P, DC, E])
        b1_sb = sb("b1_sb", [P, E, HC])
        b2_sb = sb("b2_sb", [E, D])
        x_all = sb("x_all", [P, TT, D])
        xn2_hi = sb("xn2_hi", [P, DC, TOK], F32R)
        xn2_lo = sb("xn2_lo", [P, DC, TOK], F32R)
        gates = sb("gates", [P, TT, E])
        w_sb = sb("w_sb", [P, 6, DC, D])
        causal_sb = sb("causal_sb", [P, Q])
        causal_bf = sb("causal_bf", [P, Q], BF16)
        o_t = sb("o_t", [P, G, P])
        stats = sb("stats", [P, TT, 6])
        mean_var = sb("mean_var", [P, TT, 2])
        var_eps = sb("var_eps", [P, TT])
        rstd = sb("rstd", [P, TT])
        x1 = sb("x1", [P, D])
        xn = sb("xn", [P, D])
        xn_t = sb("xn_t", [P, DC, P])
        q2_t = sb("q2_t", [P, G, P])
        k2_t = sb("k2_t", [P, G, P])
        v2 = sb("v2", [P, D])
        qbd2 = sb("qbd2", [P, G, HG, Q])
        masked = sb("masked", [P, G * PAIRS, Q])
        own = masked[:, 0:2 * G, :]
        odd = masked[:, 2 * G:4 * G, :]
        neg_max2 = sb("neg_max2", [P, G * PAIRS])
        shift2 = sb("shift2", [P, G * PAIRS, P], BF16)
        probs2 = sb("probs2", [P, G * 512])
        o2_t = sb("o2_t", [P, G, P])
        logits = sb("logits", [P, E])
        row_max = sb("row_max", [P, 1])
        row_sum = sb("row_sum", [P, 1])
        above = sb("above", [P, E, E])
        ties = sb("ties", [P, E, E])
        rank = sb("rank", [P, E])
        earlier = sb("earlier", [P, E, E])
        gate_tile = sb("gate_tile", [P, E])
        gates_t = sb("gates_t", [E, P])

        attn = ExitStack()
        with attn:
            wk_hi = sb("wk_hi", [P, DC, D], F32R, attn)
            wk_lo = sb("wk_lo", [P, DC, D], F32R, attn)
            wv_hi = sb("wv_hi", [P, DC, D], F32R, attn)
            wv_lo = sb("wv_lo", [P, DC, D], F32R, attn)
            q_hi = sb("q_hi", [P, B, G, Q], BF16, attn)
            ctx_hi = sb("ctx_hi", [P, DC, S], F32R, attn)
            ctx_lo = sb("ctx_lo", [P, DC, S], F32R, attn)
            ctx_raw = sb("ctx_raw", [P, 2, DC, CW], F32, attn)
            k_parts = [sb(f"k_parts{i}", [P, PARTS, G, hi - lo], BF16, attn) for i, (lo, hi) in enumerate(HALVES)]
            k_rest = sb("k_rest", [P, 2, CW], F32, attn)
            v_sb = sb("v_sb", [P, KT * D], F32, attn)
            probs = sb("probs", [P, 2, G * 512], F32, attn)
            prob_sum = sb("prob_sum", [P, G * 512], F32, attn)
            qbd = sb("qbd", [P, G, HG, Q], BF16, attn)
            q_stack = sb("q_stack", [STACK + 1, 2, HG, G, Q], BF16, attn)
            maxes = sb("maxes", [P, G * PAIRS, NC], F32, attn)
            neg_max = sb("neg_max", [P, G * PAIRS], F32, attn)
            shift = sb("shift", [P, G * PAIRS, P], BF16, attn)
            pro = ExitStack()
            with pro:
                w_raw = sb("w_raw", [P, 2, DC, D], F32, pro)
                xn_all = sb("xn_all", [P, TT, D], F32, pro)
                xn_all_t = sb("xn_all_t", [P, DC, TOK], F32, pro)
                q_rest = sb("q_rest", [P, B, G, Q], F32, pro)
                q_mid = sb("q_mid", [P, B, G, Q], BF16, pro)
                q_lo = sb("q_lo", [P, B, G, Q], BF16, pro)
            SHARED = -(-5 * TOK * G * 4 // (S * 2))
            k_stack = sb("k_stack", [STACK + 1, HG * G, S], BF16, attn)
        moe = ExitStack()
        with moe:
            raw_0 = sb("raw_0", [P, 2, DC * HID], F32, moe)
            w_hi_0 = sb("w_hi_0", [P, 2, DC * HID], F32R, moe)
            w_lo_0 = sb("w_lo_0", [P, 2, DC * HID], F32R, moe)
            h_raw = sb("h_raw", [P, 2, TOK], F32, moe)
            h_hi = sb("h_hi", [P, 4, TOK], F32R, moe)
            h_lo = sb("h_lo", [P, 4, TOK], F32R, moe)
            qbd2_alone = sb("qbd2_alone", [P, G, HG, Q], F32, moe)
            shift2_alone = sb("shift2_alone", [P, G * PAIRS, P], BF16, moe)
            raw_sb = [raw_0, sb("raw_1", [P, 2, DC * HID], F32, moe)]
            w_hi = [w_hi_0, sb("w_hi_1", [P, 2, DC * HID], F32R, moe)]
            w_lo = [w_lo_0, sb("w_lo_1", [P, 2, DC * HID], F32R, moe)]

        bank = stack.enter_context(nc.psum_tensor("bank", [P, 8, 512], F32))
        UNIT, O = 4, 7

        def key_part(part, c, g):
            i = c * 2 // NC
            lo = HALVES[i][0]
            return k_parts[i][:, part, g, EDGE[c] - lo:EDGE[c + 1] - lo]

        q_dram = nc.dram_tensor("q_dram", (STACK, HG, B, G * Q), BF16, kind="Internal").ap()
        k_dram = [nc.dram_tensor(f"k_dram{i}", (PARTS, DK, HG, G, hi - lo), BF16, kind="Internal").ap()
                  for i, (lo, hi) in enumerate(HALVES)]

        consts_in = sem("consts_in")
        late_in = sem("late_in")
        kv_weights_in = sem("kv_weights_in")
        weights_in = sem("weights_in")
        x_in = sem("x_in")
        ctx_in = [sem(f"ctx_in{i}") for i in range(2)]
        consts_made = sem("consts_made")
        exponent_made = sem("exponent_made")
        kv_weights_split = sem("kv_weights_split")
        stats_ready = sem("stats_ready")
        rstd_ready = sem("rstd_ready")
        xn_ready = sem("xn_ready")
        xt_psum = sem("xt_psum")
        xt_ready = sem("xt_ready")
        q_psum = sem("q_psum")
        q_hi_done = sem("q_hi_done")
        q_rest_done = sem("q_rest_done")
        q_mid_done = sem("q_mid_done")
        q_split = sem("q_split")
        q_saved = sem("q_saved")
        q_stacked = sem("q_stacked")
        ones_row = sem("ones_row")
        bo_psum = sem("bo_psum")
        qbd_ready = sem("qbd_ready")
        ctx_hi_done = sem("ctx_hi_done")
        ctx_lo_done = sem("ctx_lo_done")
        filled = sem("filled")
        read_act = sem("read_act")
        read_dve = sem("read_dve")
        k_hi_done = sem("k_hi_done")
        k_mid_done = sem("k_mid_done")
        k_lo_done = sem("k_lo_done")
        k_saved = [sem(f"k_saved{i}") for i in range(2)]
        k_stacked = [sem(f"k_stacked{i}") for i in range(2)]
        shift_ready = sem("shift_ready")
        scores_done = sem("scores_done")
        exp_done = sem("exp_done")
        pv_done = sem("pv_done")
        summed = sem("summed")
        denom_done = sem("denom_done")
        o_read = sem("o_read")
        o_ready = sem("o_ready")
        dve_step = sem("dve_step")
        xn1_ready = sem("xn1_ready")
        qbd2_ready = sem("qbd2_ready")
        shift2_ready = sem("shift2_ready")
        o2_ready = sem("o2_ready")
        xn2_ready = sem("xn2_ready")
        xn2_hi_done = sem("xn2_hi_done")
        negmax_ready = sem("negmax_ready")
        gates_ready = sem("gates_ready")
        tile_done = sem("tile_done")
        w_in = [sem(f"w_in{i}") for i in range(2)]
        w_hi_done = sem("w_hi_done")
        w_split = sem("w_split")
        h_psum = sem("h_psum")
        h_ready = sem("h_ready")
        h_split = sem("h_split")
        y_chunk = sem("y_chunk")
        y_taken = sem("y_taken")
        stored = sem("stored")

        block = stack.enter_context(nc.Block())

        def chunk_of_all(e, c):
            return (e + 1) * HC + c

        def is_first(b):
            return isinstance(b, int) and b == 0

        def sum_probabilities(engine, eng, b, k, s):
            n = b * KT + k
            eng.wait_ge(exp_done, n + 1)
            if k == 0:
                if not is_first(b):
                    eng.wait_ge(denom_done, b)
                acc = zero[:, 0:1].broadcast_to([P, G * 512])
            else:
                eng.wait_ge(summed, n)
                acc = prob_sum[0:ROWS[k], :]
            engine.tensor_tensor(prob_sum[0:ROWS[k], :], probs[0:ROWS[k], s % 2, :], acc[0:ROWS[k]],
                                 ALU.add).then_inc(summed, 1)

        @block.sync
        def _(sp):
            sp.dma_start(x_all[:, :, :], x).then_inc(x_in, 16)

            def load(b, c):
                if not (is_first(b) and c < 2):
                    sp.wait_ge(ctx_lo_done, b * NC + c - 1)
                sp.dma_start(ctx_raw[:, c % 2, :, 0:EDGE[c + 1] - EDGE[c]],
                             ctx_t[b, :, :, EDGE[c]:EDGE[c + 1]]).then_inc(ctx_in[c % 2], 16)

            def save_keys(b, i):
                sp.wait_ge(k_lo_done, b * K_UNITS + (i + 1) * K_UNITS // 2)
                if not is_first(b):
                    sp.wait_ge(k_stacked[i], b * 16 * len(K_STACK))
                for part in range(PARTS):
                    sp.dma_start(k_dram[i][part].rearrange("i h g k -> h i (g k)"),
                                 k_parts[i][:, part].rearrange("p g k -> p (g k)")).then_inc(k_saved[i], 16)

            def stack_keys(b, i):
                sp.wait_ge(k_saved[i], (b + 1) * 16 * PARTS)
                rows = k_dram[i].rearrange("r i h g k -> (r i) (h g) k")
                lo, hi = HALVES[i]
                at = 0
                for first, last in K_STACK:
                    sp.dma_start(k_stack[at:at + (last - first) * DK, :, lo:hi],
                                 rows[first * DK:last * DK]).then_inc(k_stacked[i], 16)
                    at += (last - first) * DK

            def load_expert(e, i):
                sp.dma_start(raw_sb[i][:, 0], w1[e]).then_inc(w_in[i], 16)
                sp.dma_start(raw_sb[i][:, 1], w2[e]).then_inc(w_in[i], 16)

            def stack_queries(b, parity):
                sp.dma_start(q_stack[0:STACK, parity].rearrange("p h g q -> p h (g q)"),
                             q_dram[:, :, bass.ds(b, 1), :].rearrange("p h b q -> p h (b q)")).then_inc(q_stacked, 16)

            sp.dma_start(w_raw[:, :, :, :], w_t[:, 6:8]).then_inc(kv_weights_in, 16)
            sp.dma_start(ident[:, :], eye).then_inc(consts_in, 16)
            load(0, 0)
            sp.dma_start(bias_sb[:, :, :], biases).then_inc(consts_in, 16)
            load(0, 1)
            for dst, src in ((bo_sb[:, :], bo_row), (bg_sb[:, :], bg_row), (wg_sb[:, :, :], wg_t),
                             (b1_sb[:, :, :], b1), (b2_sb[:, :], b2), (causal_sb[:, :], causal)):
                sp.dma_start(dst, src).then_inc(late_in, 16)
            load(0, 2)
            load(0, 3)
            sp.wait_ge(q_split, 1)
            for r, part in enumerate(Q_STACK):
                sp.dma_start(q_dram[r * DK:(r + 1) * DK].rearrange("i h b q -> h i (b q)"),
                             (q_hi, q_mid, q_lo)[part][:, :, :, :].rearrange("p b g q -> p (b g q)")).then_inc(q_saved, 16)
            sp.wait_ge(q_saved, 16 * len(Q_STACK))
            stack_queries(0, 0)

            load(1, 0)
            load(1, 1)
            save_keys(0, 0)
            save_keys(0, 1)
            load(1, 2)
            stack_keys(0, 0)
            load(1, 3)

            def tile(t, more):
                for s in range(STEPS):
                    bi, k = divmod(s, KT)
                    b = 2 * t + bi
                    if k == 0:
                        if not is_first(b):
                            sp.wait_ge(scores_done, b * KT)
                        stack_keys(b, 1)
                        if more > bi:
                            stack_queries(b + 1, (bi + 1) % 2)
                    elif k == LAST_V_AT + 1 and more == bi == 1:
                        sp.wait_ge(scores_done, b * KT + k + 1)
                        load_expert(0, 0)
                    elif k == 2 and more > bi:
                        save_keys(b + 1, 0)
                    elif k == 5 and more > bi:
                        save_keys(b + 1, 1)
                    elif k == 7 and more > bi:
                        sp.wait_ge(scores_done, b * KT + -(-HALVES[0][1] // P))
                        stack_keys(b + 1, 0)
                    if k in LOAD_AT and more == 2:
                        load(b + 2, LOAD_AT.index(k))

            tile(0, 2)
            with sp.Fori(1, TT - 1) as t:
                tile(t, 2)
            tile(TT - 1, 1)
            sp.wait_ge(denom_done, B)
            load_expert(1, 1)
            with sp.Fori(1, E // 2) as p:
                for i in range(2):
                    sp.wait_ge(w_split, (2 * p + i - 1) * 2 * PIECES)
                    load_expert(2 * p + i, i)
            sp.wait_ge(y_taken, E + 1)
            sp.dma_start(out, x_all[:, :, :]).then_inc(stored, 16)
            sp.wait_ge(stored, 16)

        @block.gpsimd
        def _(pool):
            nc.gpsimd.memset(zero[:, :], 0.0).then_inc(consts_made, 1)
            nc.gpsimd.memset(neg_half[:, :], -0.5).then_inc(exponent_made, 1)
            nc.gpsimd.memset(ones_bf[:, :], 1.0).then_inc(consts_made, 1)
            nc.gpsimd.memset(ones_f[:, :], 1.0).then_inc(consts_made, 1)
            pool.dma_start(mask_sb[:, :], masks).then_inc(weights_in, 16)
            pool.dma_start(w_sb[:, 0], w_t[:, 0]).then_inc(weights_in, 16)
            pool.dma_start(w_sb[:, 1:6], w_t[:, 1:6]).then_inc(weights_in, 16)
            pool.wait_ge(exponent_made, 1)

            def inverse_root(n, width=1):
                pool.wait_ge(stats_ready, n)
                nc.gpsimd.tensor_tensor(rstd[:, 0:width], var_eps[:, 0:width], neg_half[:, 0:width],
                                        ALU.pow).then_inc(rstd_ready, 1)

            def spread_queries(b):
                nc.gpsimd.tensor_tensor(
                    qbd[:, :, :, :],
                    q_hi[:, bass.ds(b, 1)].rearrange("p b g q -> p (b g) q").unsqueeze(2).broadcast_to([P, G, HG, Q]),
                    mask_sb[:, 0:HG].unsqueeze(1).unsqueeze(3).broadcast_to([P, G, HG, Q]),
                    ALU.mult).then_inc(qbd_ready, 1)

            inverse_root(1, TT)
            pool.wait_ge(rstd_ready, 1)
            nc.gpsimd.memset(k_stack[STACK:STACK + 1, SHARED:, :], 1.0).then_inc(ones_row, 1)
            pool.wait_ge(consts_made, CONSTS_MADE)
            pool.wait_ge(weights_in, 48)
            pool.wait_ge(q_hi_done, G)
            pool.wait_ge(ones_row, 1)
            spread_queries(0)
            pool.wait_ge(qbd_ready, 1)
            pool.wait_ge(kv_weights_split, 2)
            pool.wait_ge(q_saved, 16 * len(Q_STACK))
            nc.gpsimd.memset(k_stack[STACK:STACK + 1, 0:SHARED, :], 1.0).then_inc(ones_row, 1)

            def tile(t, more, chain):
                for s in range(STEPS):
                    bi, k = divmod(s, KT)
                    b = 2 * t + bi
                    if not more == bi == 1:
                        sum_probabilities(nc.gpsimd, pool, b, k, s)
                    if k == 0 and more > bi:
                        spread_queries(b + 1)
                    if "y1" in chain.get(s, []):
                        inverse_root(2 * t)
                    if "y2" in chain.get(s, []):
                        inverse_root(2 * t + 1)

            tile(0, 2, {})
            with pool.Fori(1, TT - 1) as t:
                tile(t, 2, CHAIN_AT)
            tile(TT - 1, 1, CHAIN_AT_LAST)
            inverse_root(2 * TT)
            inverse_root(2 * TT + 1)

        @block.scalar
        def _(act):
            def split_hi(b, c):
                act.wait_ge(ctx_in[c % 2], 16 * (2 * b + c // 2 + 1))
                nc.scalar.activation(ctx_hi[:, :, EDGE[c]:EDGE[c + 1]], ctx_raw[:, c % 2, :, 0:EDGE[c + 1] - EDGE[c]],
                                     ACT.Copy).then_inc(ctx_hi_done, 1)

            def middle_parts(units, s, b):
                for n, kind, u in units.at[s]:
                    if kind == "K":
                        c, g = divmod(u, G)
                        act.wait_ge(read_dve, units.before[2] + units.counts(n + 1)[2])
                        nc.scalar.activation(key_part(1, c, g), k_rest[:, u % 2, 0:EDGE[c + 1] - EDGE[c]],
                                             ACT.Copy).then_inc(k_mid_done, 1)

            def unit(units, n, kind, u, t, b, parity):
                if kind == "M" or kind in ("y1", "s0", "s1", "o0", "o1", "y2", "b2"):
                    return
                src = bank[:, UNIT + n % RING, :]
                units.wait_filled(act, filled, n)
                if kind == "K":
                    c, g = divmod(u, G)
                    if not is_first(b) and u % (K_UNITS // 2) == 0:
                        act.wait_ge(k_saved[2 * u // K_UNITS], b * 16 * PARTS)
                    nc.scalar.activation(key_part(0, c, g), src[:, EDGE[c] - CH[c]:CW],
                                         ACT.Identity, bias=bias_sb[:, 1, g:g + 1]).then_inc(k_hi_done, 1)
                elif kind in ("V", "VL"):
                    nc.scalar.activation(v_sb[0:ROWS[u], u * D:u * D + D], src[0:ROWS[u], 0:D],
                                         ACT.Copy).then_inc(read_act, 1)
                elif kind == "X":
                    nc.scalar.activation(q_stack[STACK:STACK + 1, parity, :, u, :],
                                         src[STACK:STACK + 1, :].rearrange("p (h q) -> p h q", h=HG),
                                         ACT.Copy).then_inc(read_act, 1)
                elif kind == "xt1":
                    nc.scalar.activation(xn_t[:, :, :].rearrange("p c n -> p (c n)"), src[:, 0:D],
                                         ACT.Copy).then_inc(read_act, 1)
                elif kind == "qk":
                    nc.scalar.activation(k2_t[:, :, :], src[:, G * P:2 * G * P].rearrange("p (g n) -> p g n", g=G),
                                         ACT.Copy)
                    nc.scalar.activation(q2_t[:, :, :], src[:, 0:G * P].rearrange("p (g n) -> p g n", g=G),
                                         ACT.Copy, scale=SCALE).then_inc(read_act, 1)
                elif kind == "v":
                    nc.scalar.activation(v2[:, :], src[:, 0:D], ACT.Copy).then_inc(read_act, 1)
                elif kind.startswith("st"):
                    bi, g = int(kind[2]), int(kind[3])
                    rows = slice(bi * Q, bi * Q + Q)
                    nc.scalar.activation(probs2[rows, g * 512:g * 512 + 512], src[rows, :], ACT.Exp)\
                        .then_inc(read_act, 1)
                elif kind == "xt2":
                    nc.scalar.activation(xn_t[:, :, :].rearrange("p c n -> p (c n)"), src[:, 0:D],
                                         ACT.Copy).then_inc(read_act, 1)
                    act.wait_ge(read_act, units.before[1] + units.counts(n + 1)[1])
                    nc.scalar.activation(xn2_hi[:, :, bass.ds(t * P, P)], xn_t[:, :, :], ACT.Copy)\
                        .then_inc(xn2_hi_done, 1)
                elif kind == "router":
                    act.wait_ge(negmax_ready, t + 1)
                    nc.scalar.activation(logits[:, :], src[:, 0:E], ACT.Exp, bias=row_max[:, :],
                                         accum_out=row_sum[:, :]).then_inc(read_act, 1)
                elif kind == "gt":
                    nc.scalar.activation(gates_t[:, :], src[0:E, 0:P], ACT.Copy).then_inc(read_act, 1)

            def step(units, s, t, b, parity):
                for late in (False, True):
                    for n, kind, u in units.at[s]:
                        if (kind in AFTER_WEIGHING) == late and not (kind == "X" and units is not PROLOGUE):
                            unit(units, n, kind, u, t, b, parity)
                    if not late:
                        middle_parts(units, s, b)

            def prepare(k):
                for b, c in FIRST_SPLIT.get(k, []) if k else []:
                    split_hi(b, c)
                step(PROLOGUE, k, 0, 0, 0)

            for b, c in FIRST_SPLIT[0]:
                split_hi(b, c)
            act.wait_ge(consts_in, CONST_DMAS * 16)
            act.wait_ge(consts_made, CONSTS_MADE)
            act.wait_ge(xt_psum, 1)
            nc.scalar.activation(xn_all_t[:, :, :], bank[:, 0:DC, :], ACT.Copy).then_inc(xt_ready, 1)
            prepare(0)
            act.wait_ge(q_psum, 1)
            for g in range(G):
                nc.scalar.activation(q_hi[:, :, g, :], bank[:, 2 + g, :].rearrange("p (b q) -> p b q", b=B),
                                     ACT.Identity, bias=bias_sb[:, 0, g:g + 1]).then_inc(q_hi_done, 1)
            act.wait_ge(q_rest_done, G)
            nc.scalar.activation(q_mid[:, :, :, :], q_rest[:, :, :, :], ACT.Copy).then_inc(q_mid_done, 1)
            for k in range(1, FIRST_STEPS):
                prepare(k)

            def split_w(i, count, j):
                w, part = divmod(j, PIECES)
                if j == 0:
                    act.wait_ge(w_in[i], count)
                at = slice(part * PIECE, part * PIECE + PIECE)
                nc.scalar.activation(w_hi[i][:, w, at], raw_sb[i][:, w, at], ACT.Copy).then_inc(w_hi_done, 1)

            def gelu(e, c, n, at, width, wait):
                act.wait_ge(h_psum, n + 1)
                if wait:
                    act.wait_ge(h_split, n - 1)
                nc.scalar.activation(h_raw[:, c % 2, 0:width], bank[:, at, 0:width],
                                     ACT.Gelu, bias=b1_sb[:, bass.ds(e, 1), c:c + 1].rearrange("p a b -> p (a b)"))\
                    .then_inc(h_ready, 1)

            def tile(t, units, more):
                for s in range(STEPS):
                    bi, k = divmod(s, KT)
                    b = 2 * t + bi
                    n = b * KT + k
                    if k == SHIFT_AT:
                        for m, kind, u in units.at[s][:units.ahead[s]]:
                            unit(units, m, kind, u, t - 1, b + 1, (bi + 1) % 2)
                    act.wait_ge(scores_done, n + 1)
                    if not (is_first(b) and k < 2):
                        act.wait_ge(pv_done, n - 1)
                        act.wait_ge(summed, n - 1)
                    nc.scalar.activation(probs[0:ROWS[k], s % 2, :].rearrange("p (g n) -> p g n", g=G),
                                         bank[0:ROWS[k], 2 * (s % 2):2 * (s % 2) + 2, :], ACT.Exp,
                                         scale=SCALE).then_inc(exp_done, 1)
                    step(units, s, t - 1, b + 1, (bi + 1) % 2)
                    if more == bi == 1 and k in SPLIT_W_AT:
                        split_w(0, 32, SPLIT_W_AT.index(k))
                    if k in SPLIT_AT and (more == 2 or more > bi and SPLIT_AT[k][0] == 1):
                        split_hi(b + SPLIT_AT[k][0], SPLIT_AT[k][1])

            tile(0, FIRST, 2)
            with act.Fori(1, TT - 1) as t:
                tile(t, MIDDLE(t), 2)
            tile(TT - 1, LAST, 1)

            act.wait_ge(late_in, LATE_DMAS * 16)
            for s in range(STEPS):
                for m, kind, u in TAIL.at[s]:
                    unit(TAIL, m, kind, u, TT - 1, B, 0)
                if s in FIRST_EXPERT_AT:
                    c = FIRST_EXPERT_AT.index(s)
                    gelu(0, c, c, c % 2, HALF * P, c >= 2)

            def experts(p, more):
                for i in range(2):
                    e = 2 * p + i
                    for c in range(HC):
                        gelu(e, c, chunk_of_all(e, c), c % 4, HALF * P if is_first(p) and i == 0 else TOK, True)
                        if i == 0 or more:
                            if c == PIECES and not (is_first(p) and i == 0):
                                act.wait_ge(y_chunk, chunk_of_all(e, 0))
                            split_w((i + 1) % 2, 32 * (p + 1 + i), c)

            experts(0, True)
            with act.Fori(1, E // 2 - 1) as p:
                experts(p, True)
            experts(E // 2 - 1, False)

        @block.vector
        def _(dve):
            links = [0, 0]

            def link(ins):
                links[0] += 1
                ins.then_inc(dve_step, 1)
                dve.wait_ge(dve_step, links[1] + links[0])

            def statistics(src, at=0):
                link(nc.vector.bn_stats(stats[:, at, :], src))
                nc.vector.memset(unused[:, :], 0.0)
                link(nc.vector.bn_aggr(mean_var[:, at, :], stats[:, at, :]))

            def normalize(dst, src, n, done, at=0):
                dve.wait_ge(rstd_ready, n)
                nc.vector.tensor_scalar(dst, src, mean_var[:, at, 0:1], rstd[:, at:at + 1], ALU.subtract,
                                        ALU.mult).then_inc(done, 1)

            def split_lo(b, c):
                dve.wait_ge(ctx_hi_done, b * NC + c + 1)
                nc.vector.tensor_tensor(ctx_lo[:, :, EDGE[c]:EDGE[c + 1]], ctx_raw[:, c % 2, :, 0:EDGE[c + 1] - EDGE[c]],
                                        ctx_hi[:, :, EDGE[c]:EDGE[c + 1]].bitcast(F32),
                                        ALU.subtract).then_inc(ctx_lo_done, 1)

            def own_heads(src, read, count):
                both = src.rearrange("p (w s q) -> p w s q", w=2 * G, s=2)
                link(nc.vector.tensor_scalar(odd, both[:, :, 1, :], mask_sb[:, HG + 1:HG + 2], None, ALU.mult))
                nc.vector.scalar_tensor_tensor(out=own, in0=both[:, :, 0, :], scalar=mask_sb[:, HG:HG + 1],
                                               in1=odd, op0=ALU.mult, op1=ALU.add).then_inc(read, 1)
                dve.wait_ge(read, count)

            def divide_heads(dst, done):
                link(nc.vector.reciprocal(own[:, G:2 * G, :], own[:, G:2 * G, :]))
                nc.vector.tensor_tensor(dst, own[:, 0:G, :], own[:, G:2 * G, :], ALU.mult).then_inc(done, 1)

            def on_diagonal(dst, values, done):
                nc.vector.tensor_tensor(dst, ident[:, :].unsqueeze(1).broadcast_to([P, G * PAIRS, P]),
                                        values.unsqueeze(2).broadcast_to([P, G * PAIRS, P]), ALU.mult).then_inc(done, 1)

            def spread_own_queries(bi, dst):
                nc.vector.tensor_tensor(
                    dst[:, :, :, :], q2_t[:, :, bi * Q:bi * Q + Q].unsqueeze(2).broadcast_to([P, G, HG, Q]),
                    mask_sb[:, 0:HG].unsqueeze(1).unsqueeze(3).broadcast_to([P, G, HG, Q]),
                    ALU.mult).then_inc(qbd2_ready, 1)

            def unit(units, n, kind, u, t, b):
                src = bank[:, UNIT + n % RING, :]
                if kind == "K":
                    c, g = divmod(u, G)
                    if not (is_first(b) and u < 2):
                        dve.wait_ge(k_lo_done, b * K_UNITS + u - 1)
                    dve.wait_ge(k_hi_done, b * K_UNITS + u + 1)
                    nc.vector.scalar_tensor_tensor(
                        out=k_rest[:, u % 2, 0:EDGE[c + 1] - EDGE[c]], in0=src[:, EDGE[c] - CH[c]:CW],
                        scalar=bias_sb[:, 1, g:g + 1], in1=key_part(0, c, g),
                        op0=ALU.add, op1=ALU.subtract).then_inc(read_dve, 1)
                elif kind == "router":
                    units.wait_filled(dve, filled, n)
                    nc.vector.tensor_reduce(row_max[:, :], src[:, 0:E], AX.X, ALU.max, negate=True)\
                        .then_inc(negmax_ready, 1)
                elif kind == "xt2":
                    dve.wait_ge(xn2_hi_done, t + 1)
                    nc.vector.tensor_tensor(xn2_lo[:, :, bass.ds(t * P, P)], xn_t[:, :, :],
                                            xn2_hi[:, :, bass.ds(t * P, P)].bitcast(F32), ALU.subtract)
                if kind in READ_BY_ACT or kind == "K":
                    return
                units.wait_filled(dve, filled, n)
                if kind == "M":
                    c, pair = divmod(u, G * PAIRS)
                    nc.vector.tensor_reduce(maxes[:, pair, c:c + 1], src[:, 0:EDGE[c + 1] - EDGE[c]], AX.X,
                                            ALU.max).then_inc(read_dve, 1)
                elif kind in ("y1", "y2"):
                    x_tile = x_all[:, bass.ds(t, 1), :].rearrange("p a n -> p (a n)")
                    nc.vector.tensor_tensor(x1[:, :], src[:, 0:D], x_tile if kind == "y1" else x1[:, :],
                                            ALU.add).then_inc(read_dve, 1)
                elif kind in ("s0", "s1"):
                    nc.vector.tensor_tensor(masked[:, :, :], src.rearrange("p (n k) -> p n k", k=Q),
                                            causal_sb[:, :].unsqueeze(1).broadcast_to([P, G * PAIRS, Q]),
                                            ALU.add).then_inc(read_dve, 1)
                elif kind in ("o0", "o1"):
                    bi = int(kind[1])
                    own_heads(src, read_dve, units.before[2] + units.counts(n + 1)[2])
                    divide_heads(o2_t[:, :, bi * Q:bi * Q + Q], o2_ready)
                elif kind == "b2":
                    x_tile = x_all[:, bass.ds(t, 1), :].rearrange("p a n -> p (a n)")
                    nc.vector.tensor_tensor(x_tile, x1[:, :], src[:, 0:D], ALU.add).then_inc(read_dve, 1)
                    nc.vector.memset(unused[:, :], 0.0).then_inc(tile_done, 1)

            def after_units(units, s, *kinds):
                for n, kind, _ in units.at[s]:
                    if kinds and kind not in kinds:
                        continue
                    if kind in ("y1", "y2", "s0", "s1"):
                        dve.wait_ge(read_dve, units.before[2] + units.counts(n + 1)[2])
                    if kind in ("y1", "y2"):
                        statistics(x1[:, :])
                        nc.vector.tensor_scalar(var_eps[:, 0:1], mean_var[:, 0, 1:2], EPS, None,
                                                ALU.add).then_inc(stats_ready, 1)
                    elif kind in ("s0", "s1"):
                        link(nc.vector.tensor_reduce(neg_max2[:, :], masked[:, :, :], AX.X, ALU.max, negate=True))
                        on_diagonal((shift2_alone if units is TAIL and kind == "s1" else shift2)[:, :, :],
                                    neg_max2[:, :], shift2_ready)

            def route(units, t):
                units.wait_read_act(dve, read_act, "router")
                link(nc.vector.reciprocal(row_sum[:, :], row_sum[:, :]))
                link(nc.vector.tensor_scalar(logits[:, :], logits[:, :], row_sum[:, :], None, ALU.mult))
                mine = logits[:, :].unsqueeze(2).broadcast_to([P, E, E])
                other = logits[:, :].unsqueeze(1).broadcast_to([P, E, E])
                link(nc.vector.tensor_tensor(above[:, :, :], other, mine, ALU.is_gt))
                link(nc.vector.tensor_tensor(ties[:, :, :], other, mine, ALU.is_equal))
                link(nc.vector.tensor_tensor(ties[:, :, :], ties[:, :, :], earlier[:, :, :], ALU.mult))
                link(nc.vector.tensor_tensor(above[:, :, :], above[:, :, :], ties[:, :, :], ALU.add))
                link(nc.vector.tensor_reduce(rank[:, :], above[:, :, :], AX.X, ALU.add))
                nc.vector.scalar_tensor_tensor(out=gate_tile[:, :], in0=rank[:, :], scalar=1.5, in1=logits[:, :],
                                               op0=ALU.is_lt, op1=ALU.mult).then_inc(gates_ready, 1)
                dve.wait_ge(gates_ready, t + 1)
                nc.vector.tensor_copy(gates[:, bass.ds(t, 1), :].rearrange("p a n -> p (a n)"), gate_tile[:, :])

            def chain_between(units, s, t):
                before = units.chain.get(s - 1, [])
                if "y1" in before:
                    normalize(xn[:, :], x1[:, :], 2 * t + 2, xn1_ready)
                if "y2" in before:
                    normalize(xn[:, :], x1[:, :], 2 * t + 3, xn2_ready)
                if "qk" in before:
                    units.wait_read_act(dve, read_act, "qk")
                    spread_own_queries(0, qbd2)
                    if units is TAIL:
                        spread_own_queries(1, qbd2_alone)
                if "st01" in before and units is not TAIL:
                    units.wait_read_act(dve, read_act, "st01")
                    spread_own_queries(1, qbd2)
                if "router" in before:
                    route(units, t)

            dve.wait_ge(x_in, 16)
            for t in range(TT):
                statistics(x_all[:, t, :], t)
            nc.vector.tensor_scalar(var_eps[:, :], mean_var[:, :, 1], EPS, None, ALU.add).then_inc(stats_ready, 1)
            dve.wait_ge(kv_weights_in, 16)
            for w, hi, lo in ((0, wk_hi, wk_lo), (1, wv_hi, wv_lo)):
                link(nc.vector.tensor_copy(hi[:, :, :], w_raw[:, w]))
                nc.vector.tensor_tensor(lo[:, :, :], w_raw[:, w], hi[:, :, :].bitcast(F32),
                                        ALU.subtract).then_inc(kv_weights_split, 1)
            for t in range(TT):
                normalize(xn_all[:, t, :], x_all[:, t, :], 1, xn_ready, t)
            dve.wait_ge(consts_in, CONST_DMAS * 16)
            nc.vector.tensor_copy(ident_bf[:, :], ident[:, :]).then_inc(consts_made, 1)

            def low_parts(units, s, b):
                for _, kind, u in units.at[s]:
                    if kind == "K":
                        c, g = divmod(u, G)
                        dve.wait_ge(k_mid_done, b * K_UNITS + u + 1)
                        nc.vector.tensor_tensor(key_part(2, c, g), k_rest[:, u % 2, 0:EDGE[c + 1] - EDGE[c]],
                                                key_part(1, c, g), ALU.subtract).then_inc(k_lo_done, 1)

            def find_shift():
                link(nc.vector.tensor_reduce(neg_max[:, :], maxes[:, :, :], AX.X, ALU.max, negate=True))
                on_diagonal(shift[:, :, :], neg_max[:, :], shift_ready)

            def prepare(k):
                for b, c in FIRST_SPLIT.get(k, []):
                    split_lo(b, c)
                if k == FIRST_STEPS - 1:
                    dve.wait_ge(read_dve, PROLOGUE.total()[2])
                    find_shift()
                for n, kind, u in PROLOGUE.at[k]:
                    unit(PROLOGUE, n, kind, u, 0, 0)
                low_parts(PROLOGUE, k, 0)

            prepare(0)
            for g in range(G):
                dve.wait_ge(q_hi_done, g + 1)
                nc.vector.scalar_tensor_tensor(
                    out=q_rest[:, :, g, :], in0=bank[:, 2 + g, :].rearrange("p (b q) -> p b q", b=B),
                    scalar=bias_sb[:, 0, g:g + 1], in1=q_hi[:, :, g, :], op0=ALU.add,
                    op1=ALU.subtract).then_inc(q_rest_done, 1)
            dve.wait_ge(q_mid_done, 1)
            nc.vector.tensor_tensor(q_lo[:, :, :, :], q_rest[:, :, :, :], q_mid[:, :, :, :], ALU.subtract)\
                .then_inc(q_split, 1)
            for k in range(1, FIRST_STEPS):
                prepare(k)
            dve.wait_ge(late_in, LATE_DMAS * 16)
            nc.vector.tensor_copy(causal_bf[:, :], causal_sb[:, :])
            link(nc.vector.memset(earlier[:, :, :], 0.0))
            for e in range(1, E):
                nc.vector.memset(earlier[:, e, 0:e], 1.0)
            dve.wait_ge(bo_psum, 1)
            link(nc.vector.tensor_tensor(bo_all[:, :], bank[0:1, O, 0:D], bo_sb[:, :], ALU.add))

            def split_w(i, n, j):
                w, part = divmod(j, PIECES)
                at = slice(part * PIECE, part * PIECE + PIECE)
                dve.wait_ge(w_hi_done, n + 1)
                nc.vector.tensor_tensor(w_lo[i][:, w, at], raw_sb[i][:, w, at], w_hi[i][:, w, at].bitcast(F32),
                                        ALU.subtract).then_inc(w_split, 1)

            def tile(t, units, more, chain):
                for s in range(STEPS):
                    bi, k = divmod(s, KT)
                    b = 2 * t + bi
                    if more == bi == 1:
                        sum_probabilities(nc.vector, dve, b, k, s)
                    if k == 1 and not is_first(b):
                        dve.wait_ge(denom_done, b)
                        at = (bi + 1) % 2 * Q
                        own_heads(bank[:, O, :], o_read, b)
                    if k == SHIFT_AT - 1 and more > bi:
                        n = max(n for j in range(s) for n, kind, _ in units.at[j] if kind == "M")
                        dve.wait_ge(read_dve, units.before[2] + units.counts(n + 1)[2])
                        find_shift()
                    for m, kind, u in units.at[s]:
                        unit(units, m, kind, u, t - 1, b + 1)
                    if k == 1 and not is_first(b):
                        divide_heads(o_t[:, :, at:at + Q], o_ready)
                    after_units(units, s)
                    low_parts(units, s, b + 1)
                    if chain:
                        chain_between(units, s, t - 1)
                    if k - 1 in SPLIT_AT and (more == 2 or more > bi and SPLIT_AT[k - 1][0] == 1):
                        split_lo(b + SPLIT_AT[k - 1][0], SPLIT_AT[k - 1][1])
                    if more == bi == 1 and k in SPLIT_W_AT:
                        split_w(0, SPLIT_W_AT.index(k), SPLIT_W_AT.index(k))

            tile(0, FIRST, 2, False)
            start = links[0]
            with dve.Fori(1, TT - 1) as t:
                links[0] = start
                links[1] = (t - 1) * TILE_LINKS
                tile(t, MIDDLE(t), 2, True)
            assert links[0] == start + TILE_LINKS, links[0] - start
            links[:] = [start + (TT - 2) * TILE_LINKS, 0]
            tile(TT - 1, LAST, 1, True)
            dve.wait_ge(denom_done, B)
            own_heads(bank[:, O, :], o_read, B)
            divide_heads(o_t[:, :, Q:2 * Q], o_ready)

            def gated_sum(e, first, last, at):
                for t in range(first, last):
                    ins = nc.vector.scalar_tensor_tensor(
                        out=x_all[:, t, :], in0=bank[:, at + t // 2, (t % 2) * D:(t % 2) * D + D],
                        scalar=gates[:, t, bass.ds(e, 1)], in1=x_all[:, t, :], op0=ALU.mult, op1=ALU.add)
                ins.then_inc(y_taken, 1)

            def split_h(c, n, width, wait):
                dve.wait_ge(h_ready, n + 1)
                if wait:
                    dve.wait_ge(y_chunk, n - 3)
                link(nc.vector.tensor_copy(h_hi[:, c % 4, 0:width], h_raw[:, c % 2, 0:width]))
                nc.vector.tensor_tensor(h_lo[:, c % 4, 0:width], h_raw[:, c % 2, 0:width],
                                        h_hi[:, c % 4, 0:width].bitcast(F32), ALU.subtract).then_inc(h_split, 1)

            for s in range(STEPS):
                for m, kind, u in TAIL.at[s]:
                    unit(TAIL, m, kind, u, TT - 1, B)
                    if kind == "s0":
                        after_units(TAIL, s, "s0")
                after_units(TAIL, s, "y1", "y2", "s1")
                chain_between(TAIL, s, TT - 1)
                if s in FIRST_EXPERT_AT:
                    c = FIRST_EXPERT_AT.index(s)
                    split_h(c, c, HALF * P, c >= 4)
                elif s == FIRST_EXPERT_AT[-1] + 3:
                    dve.wait_ge(y_chunk, HC)
                    gated_sum(0, 0, HALF, 3)

            def experts(p, more):
                for i in range(2):
                    e = 2 * p + i
                    half = is_first(p) and i == 0
                    for c in range(HC):
                        split_h(c, chunk_of_all(e, c), HALF * P if half else TOK, True)
                        if i == 0 or more:
                            split_w((i + 1) % 2, (e + 1) * 2 * PIECES + c, c)
                        if c == 2 and not half:
                            dve.wait_ge(y_chunk, chunk_of_all(e, 0))
                            gated_sum(e - 1, HALF if is_first(p) else 0, TT, 4 + 2 * ((i + 1) % 2))

            experts(0, True)
            start = links[0]
            per = 2 * HC
            with dve.Fori(1, E // 2 - 1) as p:
                links[0] = start
                links[1] = (p - 1) * per
                experts(p, True)
            links[:] = [start + (E // 2 - 2) * per, 0]
            experts(E // 2 - 1, False)
            dve.wait_ge(y_chunk, chunk_of_all(E, 0))
            gated_sum(E - 1, 0, TT, 6)

        @block.tensor
        def _(pe):
            def split_product(dst, pairs, start=True, stop=True, **more):
                n = 0
                for (a_hi, a_lo), (b_hi, b_lo) in pairs:
                    for lhs, rhs in ((a_hi, b_hi), (a_hi, b_lo), (a_lo, b_hi)):
                        n += 1
                        last = nc.tensor.matmul(dst, lhs, rhs, start=(start and n == 1),
                                                stop=(stop and n == 3 * len(pairs)), **more)
                return last

            def weigh_heads(dst_bank, at, lhs, p_rows, start, stop):
                for g in range(G):
                    for j in range(PAIRS):
                        ins = nc.tensor.matmul(dst_bank[32 * j:32 * j + 32, (at + g) * P:(at + g + 1) * P], lhs(g, j),
                                               p_rows[:, (g * PAIRS + j) * P:(g * PAIRS + j + 1) * P],
                                               start=(start and g == 0), stop=stop, skip_group_check=True)
                return ins

            def transposes(dst):
                for c in range(DC):
                    ins = nc.tensor.transpose(dst[:, c * P:c * P + P], xn[:, c * P:c * P + P], ident[:, :])
                return ins

            def unit(units, n, kind, u, t, b, parity):
                dst = bank[:, UNIT + n % RING, :]
                units.wait_free(pe, read_act, read_dve, n)
                if kind == "K":
                    c, g = divmod(u, G)
                    pe.wait_ge(ctx_lo_done, b * NC + c + 1)
                    cols, keys = slice(g * P, g * P + P), slice(CH[c], CH[c] + CW)
                    ins = split_product(dst[:, 0:CW], [((wk_hi[:, d, cols], wk_lo[:, d, cols]),
                                                        (ctx_hi[:, d, keys], ctx_lo[:, d, keys])) for d in range(DC)])
                elif kind == "X":
                    if u == 0:
                        pe.wait_ge(shift_ready, b + 1)
                    ins = nc.tensor.matmul(dst[STACK:P, :], ones_bf[:, 0:P - STACK],
                                           shift[:, u * PAIRS:(u + 1) * PAIRS].rearrange("p j c -> p (j c)"),
                                           start=True, stop=True)
                elif kind in ("V", "VL"):
                    keys = slice(u * P, u * P + ROWS[u])
                    if kind == "V":
                        c = next(c for c in range(NC) if EDGE[c + 1] >= keys.stop)
                        pe.wait_ge(ctx_lo_done, b * NC + c + 1)
                    ins = split_product(dst[0:ROWS[u], 0:D], [((ctx_hi[:, d, keys], ctx_lo[:, d, keys]),
                                                               (wv_hi[:, d, :], wv_lo[:, d, :])) for d in range(DC)])
                elif kind == "M":
                    c, pair = divmod(u, G * PAIRS)
                    g, j = divmod(pair, PAIRS)
                    if pair == 0:
                        pe.wait_ge(k_hi_done, b * K_UNITS + G * (c + 1))
                        pe.wait_ge(qbd_ready, b + 1)
                    ins = nc.tensor.matmul(dst[:, 0:EDGE[c + 1] - EDGE[c]],
                                           qbd[:, g, 2 * j:2 * j + 2, :].rearrange("p s q -> p (s q)"),
                                           key_part(0, c, g), start=True, stop=True)
                elif kind == "y1":
                    pe.wait_ge(o_ready, 2 * t + 2)
                    for g in range(G):
                        nc.tensor.matmul(dst[:, 0:D], o_t[:, g, :], w_sb[:, 1, g, :], start=(g == 0), stop=False)
                    ins = nc.tensor.matmul(dst[:, 0:D], ones_f[0:1, :], bo_all[:, :], start=False, stop=True)
                elif kind == "xt1":
                    pe.wait_ge(xn1_ready, t + 1)
                    ins = transposes(dst)
                elif kind == "qk":
                    units.wait_read_act(pe, read_act, "xt1")
                    for w in range(2):
                        for g in range(G):
                            for c in range(DC):
                                ins = nc.tensor.matmul(dst[:, (w * G + g) * P:(w * G + g + 1) * P],
                                                       w_sb[:, 2 + w, c, g * P:g * P + P], xn_t[:, c, :],
                                                       start=(c == 0), stop=(c == DC - 1))
                elif kind == "v":
                    for c in range(DC):
                        ins = nc.tensor.matmul(dst[:, 0:D], xn_t[:, c, :], w_sb[:, 4, c, :], start=(c == 0),
                                               stop=(c == DC - 1))
                elif kind in ("s0", "s1"):
                    bi = int(kind[1])
                    own_queries = qbd2_alone if units is TAIL and bi else qbd2
                    pe.wait_ge(qbd2_ready, 2 * t + bi + 1)
                    units.wait_read_act(pe, read_act, "qk")
                    for g in range(G):
                        for j in range(PAIRS):
                            m = g * PAIRS + j
                            ins = nc.tensor.matmul(dst[:, m * Q:m * Q + Q],
                                                   own_queries[:, g, 2 * j:2 * j + 2, :].rearrange("p s q -> p (s q)"),
                                                   k2_t[:, g, bi * Q:bi * Q + Q], start=True, stop=True)
                elif kind.startswith("st"):
                    bi, g = int(kind[2]), int(kind[3])
                    pe.wait_ge(shift2_ready, 2 * t + bi + 1)
                    half = dst[bi * Q:bi * Q + Q, :]
                    own_queries, shifts = (qbd2_alone, shift2_alone) if units is TAIL and bi else (qbd2, shift2)
                    nc.tensor.matmul(half, k2_t[:, g, bi * Q:bi * Q + Q], own_queries[:, g].rearrange("p h q -> p (h q)"),
                                     start=True, stop=False)
                    nc.tensor.matmul(half, ones_bf[:, 0:Q],
                                     shifts[:, g * PAIRS:(g + 1) * PAIRS].rearrange("p j c -> p (j c)"),
                                     start=False, stop=False)
                    ins = nc.tensor.matmul(half, causal_bf[:, :], ident_bf[:, :].unsqueeze(1).broadcast_to([P, PAIRS, P]),
                                           start=False, stop=True)
                elif kind in ("o0", "o1"):
                    bi = int(kind[1])
                    rows = slice(bi * Q, bi * Q + Q)
                    units.wait_read_act(pe, read_act, f"st{bi}1")
                    nc.tensor.matmul(dst[:, 0:E], ones_bf[:, :], ident_bf[:, 0:E], start=True, stop=True)
                    weigh_heads(dst, 0, lambda g, j: v2[rows, g * P + 32 * j:g * P + 32 * j + 32], probs2[rows, :],
                                True, True)
                    ins = weigh_heads(dst, G, lambda g, j: ones_f[rows, 0:32], probs2[rows, :], False, True)
                elif kind == "y2":
                    pe.wait_ge(o2_ready, 2 * (t + 1))
                    for g in range(G):
                        ins = nc.tensor.matmul(dst[:, 0:D], o2_t[:, g, :], w_sb[:, 5, g, :], start=(g == 0),
                                               stop=(g == G - 1))
                elif kind == "xt2":
                    pe.wait_ge(xn2_ready, t + 1)
                    ins = transposes(dst)
                elif kind == "router":
                    units.wait_read_act(pe, read_act, "xt2")
                    for c in range(DC):
                        nc.tensor.matmul(dst[:, 0:E], xn_t[:, c, :], wg_sb[:, c, :], start=(c == 0), stop=False)
                    ins = nc.tensor.matmul(dst[:, 0:E], ones_f[0:1, :], bg_sb[:, :], start=False, stop=True)
                elif kind == "gt":
                    pe.wait_ge(gates_ready, t + 1)
                    ins = nc.tensor.transpose(dst[0:E, 0:P], gate_tile[:, :], ident[:, :])
                elif kind == "b2":
                    units.wait_read_act(pe, read_act, "gt")
                    ins = nc.tensor.matmul(dst[:, 0:D], gates_t[:, :], b2_sb[:, :], start=True, stop=True)
                ins.then_inc(filled, 1)

            def scores(units, b, bi, k):
                n = b * KT + k
                rows, buf = ROWS[k], (KT * bi + k) % 2
                if not (is_first(b) and k < 2):
                    pe.wait_ge(exp_done, n - 1)
                if k == 0:
                    pe.wait_ge(q_stacked, (b + 1) * 16)
                    units.wait_shift(pe, read_act, bi)
                    pe.wait_ge(k_stacked[0], (b + 1) * 16 * len(K_STACK))
                if k == HALVES[0][1] // P:
                    pe.wait_ge(k_stacked[1], (b + 1) * 16 * len(K_STACK))
                for g in range(G):
                    for h in range(HG):
                        ins = nc.tensor.matmul(bank[0:rows, 2 * buf + g, h * Q:h * Q + Q],
                                               k_stack[:, h * G + g, k * P:k * P + rows], q_stack[:, bi, h, g, :],
                                               start=True, stop=True)
                ins.then_inc(scores_done, 1)

            def weigh(b, bi, k):
                n = b * KT + k
                buf = (KT * bi + k) % 2
                pe.wait_ge(exp_done, n + 1)
                if k == 0 and not is_first(b):
                    pe.wait_ge(o_read, b)
                rows = slice(0, ROWS[k])
                weigh_heads(bank[:, O, :], 0, lambda g, j: v_sb[rows, k * D + g * P + 32 * j:k * D + g * P + 32 * j + 32],
                            probs[rows, buf, :], k == 0, k == KT - 1).then_inc(pv_done, 1)

            def denominators(b):
                pe.wait_ge(summed, (b + 1) * KT)
                weigh_heads(bank[:, O, :], G, lambda g, j: ones_f[:, 0:32], prob_sum[:, :], False, True)\
                    .then_inc(denom_done, 1)

            def prepare(k):
                for n, kind, u in PROLOGUE.at[k]:
                    unit(PROLOGUE, n, kind, u, 0, 0, 0)

            pe.wait_ge(consts_in, CONST_DMAS * 16)
            pe.wait_ge(consts_made, CONSTS_MADE)
            pe.wait_ge(xn_ready, TT)
            for t in range(TT):
                for c in range(DC):
                    ins = nc.tensor.transpose(bank[:, c, t * P:t * P + P], xn_all[:, t, c * P:c * P + P], ident[:, :])
            ins.then_inc(xt_psum, 1)
            pe.wait_ge(kv_weights_split, 2)
            prepare(0)
            pe.wait_ge(weights_in, 48)
            pe.wait_ge(xt_ready, 1)
            for g in range(G):
                for c in range(DC):
                    ins = nc.tensor.matmul(bank[:, 2 + g, :], w_sb[:, 0, c, g * P:g * P + P], xn_all_t[:, c, :],
                                           start=(c == 0), stop=(c == DC - 1))
            ins.then_inc(q_psum, 1)
            for c in range(DC):
                ins = nc.tensor.matmul(bank[0:1, O, 0:D], bias_sb[:, 2, c:c + 1], w_sb[:, 1, c, :], start=(c == 0),
                                       stop=(c == DC - 1))
            ins.then_inc(bo_psum, 1)
            for k in range(1, FIRST_STEPS):
                prepare(k)

            def tile(t, units):
                for s in range(STEPS):
                    bi, k = divmod(s, KT)
                    b = 2 * t + bi
                    if k == 2:
                        weigh(b, bi, 0)
                    for n, kind, u in units.at[s][:units.ahead[s]]:
                        unit(units, n, kind, u, t - 1, b + 1, (bi + 1) % 2)
                    scores(units, b, bi, k)
                    if k == 1 and not is_first(b):
                        denominators(b - 1)
                    for n, kind, u in units.at[s][units.ahead[s]:]:
                        if kind not in AFTER_WEIGHING:
                            unit(units, n, kind, u, t - 1, b + 1, (bi + 1) % 2)
                    if k == 0 and not is_first(b):
                        weigh(b - 1, (bi + 1) % 2, KT - 1)
                    if k >= 2:
                        weigh(b, bi, k - 1)
                    for n, kind, u in units.at[s]:
                        if kind in AFTER_WEIGHING:
                            unit(units, n, kind, u, t - 1, b + 1, (bi + 1) % 2)

            pe.wait_ge(ones_row, 2)
            pe.wait_ge(late_in, LATE_DMAS * 16)
            tile(0, FIRST)
            with pe.Fori(1, TT - 1) as t:
                tile(t, MIDDLE(t))
            tile(TT - 1, LAST)
            weigh(B - 1, 1, KT - 1)
            denominators(B - 1)

            def hidden(i, c, at, first, last):
                w = [part[i][:, 0, :].rearrange("p (d n) -> p d n", d=DC) for part in (w_hi, w_lo)]
                cols, toks = slice(c * P, c * P + P), slice(first * P, last * P)
                split_product(bank[:, at, 0:(last - first) * P],
                              [((w[0][:, d, cols], w[1][:, d, cols]), (xn2_hi[:, d, toks], xn2_lo[:, d, toks]))
                               for d in range(DC)]).then_inc(h_psum, 1)

            def output(i, c, n, at, first, last):
                pe.wait_ge(h_split, n + 1)
                cols = slice(c * D, c * D + D)
                for t in range(first, last):
                    toks = slice((t - first) * P, (t - first) * P + P)
                    ins = split_product(bank[:, at + t // 2, (t % 2) * D:(t % 2) * D + D],
                                        [((h_hi[:, c % 4, toks], h_lo[:, c % 4, toks]),
                                          (w_hi[i][:, 1, cols], w_lo[i][:, 1, cols]))],
                                        start=(c == 0 and t % 2 == 0), stop=(c == HC - 1), skip_group_check=True)
                ins.then_inc(y_chunk, 1)

            for s in range(STEPS):
                for n, kind, u in TAIL.at[s]:
                    unit(TAIL, n, kind, u, TT - 1, B, 0)
                if s in FIRST_EXPERT_AT:
                    c = FIRST_EXPERT_AT.index(s)
                    if c == 0:
                        pe.wait_ge(w_split, 2 * PIECES)
                        pe.wait_ge(tile_done, HALF)
                    if c >= 2:
                        pe.wait_ge(h_ready, c - 1)
                    hidden(0, c, c % 2, 0, HALF)
                    if c > 0:
                        output(0, c - 1, c - 1, 3, 0, HALF)
                elif s == FIRST_EXPERT_AT[-1] + 1:
                    output(0, HC - 1, HC - 1, 3, 0, HALF)

            pe.wait_ge(tile_done, TT)
            pe.wait_ge(h_ready, HC)
            pe.wait_ge(y_taken, 1)

            def experts(p):
                for i in range(2):
                    e = 2 * p + i
                    half = is_first(p) and i == 0
                    for c in range(HC):
                        n = chunk_of_all(e, c)
                        if c == 0 and not half:
                            pe.wait_ge(w_split, e * 2 * PIECES + PIECES)
                        if not half or c >= 4:
                            pe.wait_ge(h_ready, n - 3)
                        hidden(i, c, c % 4, HALF if half else 0, TT)
                        if c >= 2:
                            if c == 2 and not half:
                                pe.wait_ge(w_split, e * 2 * PIECES + 2 * PIECES)
                            if c == 2 and not is_first(p):
                                pe.wait_ge(y_taken, e)
                            output(i, c - 2, n - 2, 4 + 2 * i, HALF if half else 0, TT)
                        elif not half:
                            output((i + 1) % 2, HC + c - 2, n - 2, 4 + 2 * ((i + 1) % 2),
                                   HALF if is_first(p) else 0, TT)

            experts(0)
            with pe.Fori(1, E // 2) as p:
                experts(p)
            for c in (HC - 2, HC - 1):
                output(1, c, chunk_of_all(E - 1, c), 6, 0, TT)


def kernel(**a):
    import numpy as np
    import concourse.bacc as bacc
    from concourse.bass_utils import run_bass_kernel_spmd

    def t(w):
        w = np.asarray(w)
        return w.T.reshape(DC, P, -1).transpose(1, 0, 2)

    f = {k: np.asarray(v) for k, v in a.items()}
    wi = f["L0_attn_in_proj_weight"]
    ctx = f["ctx_1024"].transpose(0, 2, 1).reshape(B, DC, P, S).transpose(0, 2, 1, 3)
    weights = np.stack([t(f["L0_xattn_Wq"]), t(f["L0_xattn_Wo"]), t(wi[0:D]), t(wi[D:2 * D]), t(wi[2 * D:3 * D]),
                        t(f["L0_attn_out_proj_weight"]), t(f["L0_xattn_Wk"]), t(f["L0_xattn_Wv"])], 1)
    biases = np.stack([f["L0_xattn_" + n].reshape(DC, P).T for n in ("bq", "bk", "bv")], 1)
    row = np.arange(P)
    head = (row[:, None] // DK == np.arange(HG)[None]).astype(np.float32)
    parity = (row[:, None] // DK % 2 == np.arange(2)[None]).astype(np.float32)
    hidden = np.where(np.arange(Q)[None] > (row % Q)[:, None], np.float32(FAR), np.float32(0))
    arrays = {
        "x": f["x"].reshape(TT, P, D).transpose(1, 0, 2),
        "ctx_t": ctx, "w_t": weights, "wg_t": t(f["L0_ffn_Wg"].T), "biases": biases,
        "bo_row": f["L0_xattn_bo"][None], "bg_row": f["L0_ffn_bg"][None],
        "w1": f["L0_ffn_W1"].reshape(E, DC, P, HID).transpose(0, 2, 1, 3),
        "b1": f["L0_ffn_b1"].reshape(E, HC, P).transpose(2, 0, 1),
        "w2": f["L0_ffn_W2"].reshape(E, HC, P, D).transpose(0, 2, 1, 3),
        "b2": f["L0_ffn_b2"],
        "eye": np.eye(P, dtype=np.float32), "masks": np.concatenate([head, parity], 1), "causal": hidden,
    }
    nc = bacc.Bacc("TRN2", target_bir_lowering=False, num_devices=1)
    args, feeds = [], {}
    for name, v in arrays.items():
        v = np.ascontiguousarray(v)
        feeds["in_" + name] = v
        args.append(nc.dram_tensor("in_" + name, v.shape, mybir.dt.from_np(v.dtype), kind="ExternalInput").ap())
    out = nc.dram_tensor("result", (P, TT, D), F32, kind="ExternalOutput").ap()
    perceiver_kernel(nc, *args, out)
    r = run_bass_kernel_spmd(nc, [feeds], core_ids=[0])
    return r.results[0]["result"].transpose(1, 0, 2).reshape(B, Q, D)
```
